# Optimizing a Trainium2 kernel written in Bass

```python
import numpy as np
import jax
import jax.numpy as jnp

def _softmax(x, axis=-1):
    return jax.nn.softmax(x, axis=axis)

def _gelu(x):
    return jax.nn.gelu(x, approximate=True)

def _silu(x):
    return jax.nn.silu(x)

def _sigmoid(x):
    return jax.nn.sigmoid(x)

def _layernorm(x, axis=-1, eps=1e-05):
    m = jnp.mean(x, axis=axis, keepdims=True)
    v = jnp.var(x, axis=axis, keepdims=True)
    return (x - m) / jnp.sqrt(v + eps)

def _scatter_add(tgt, idx, src, axis=0):
    return tgt.at[idx].add(src)

def _segment_sum(src, seg, n):
    return jax.ops.segment_sum(src, seg, n)
kernel_name = 'mk_flamingo_gated_d1_seqx_r8_8bcff9'

def setup_inputs(seed: int=0):
    np.random.seed(seed)
    _w = jnp.asarray

    def _rec_inputs():
        import jax
        import jax.numpy as jnp
        _rk = jax.random.key(seed)
        x = -0.0003929 + 0.9999 * jax.random.normal(jax.random.fold_in(_rk, 1), (4, 256, 512), jnp.float32)
        _lenS = 256 - jax.random.randint(jax.random.fold_in(_rk, 7), (4,), 0, max(1, 256 // 4) + 1, jnp.int32)
        _lenS2 = 1601 - jax.random.randint(jax.random.fold_in(_rk, 8), (4,), 0, max(1, 1601 // 4) + 1, jnp.int32)
        _ctx_4096P = jax.random.normal(jax.random.fold_in(_rk, 11), (4, 16, 512), jnp.float32)
        _ctx_4096c = jax.random.dirichlet(jax.random.fold_in(_rk, 511), 0.3 * jnp.ones((16,), jnp.float32), (4, 1601))
        _ctx_4096t = jnp.einsum('bsk,bkd->bsd', _ctx_4096c, _ctx_4096P)
        _ctx_4096t = _ctx_4096t * jax.lax.rsqrt(jnp.mean(jnp.square(_ctx_4096t)) + 1e-12) * 0.953939
        ctx_4096 = 2.81802e-05 + 1.00001 * (_ctx_4096t + 0.3 * jax.random.normal(jax.random.fold_in(_rk, 611), (4, 1601, 512), jnp.float32))
        _g = jax.random.normal(jax.random.fold_in(_rk, 9001), (2, 1), jnp.float32)
        _g = jnp.sign(_g) * jnp.maximum(jnp.abs(_g), 1.0) + (_g == 0) * 1.0
        g_xattn = _g[0]
        g_ffn = _g[1]
        return (x, ctx_4096, g_xattn, g_ffn)
    x, ctx_4096, g_xattn, g_ffn = _rec_inputs()

    def _L0_xattn_setup():
        import jax, jax.numpy as jnp
        import numpy as np
        HID = 512
        NHEAD = 32
        NKV = 8
        HDIM = 128
        G = NHEAD // NKV
        key = jax.random.key(seed)
        ks = jax.random.split(key, 6)
        s = 0.02
        B, L = (2, 256)
        return {'query': jax.random.normal(ks[0], (B, L, HID), jnp.float32), 'kv': jax.random.normal(ks[1], (B, L, HID), jnp.float32), 'Wq': jax.random.normal(ks[2], (HID, NHEAD * HDIM), jnp.float32) * s, 'bq': jnp.zeros((NHEAD * HDIM,), jnp.float32), 'Wkv': jax.random.normal(ks[3], (HID, 2 * NKV * HDIM), jnp.float32) * s, 'bkv': jnp.zeros((2 * NKV * HDIM,), jnp.float32), 'Wo': jax.random.normal(ks[4], (NHEAD * HDIM, HID), jnp.float32) * s, 'bo': jnp.zeros((HID,), jnp.float32)}
    _L0_xattn_all = _L0_xattn_setup()
    _L0_xattn_in = {k: v for k, v in _L0_xattn_all.items() if k in ('Wq', 'bq', 'Wkv', 'bkv', 'Wo', 'bo')}
    del _L0_xattn_all

    def _L0_ffn_setup():
        import jax, jax.numpy as jnp
        import numpy as np
        R = 16
        ALPHA = 32
        SCALING = ALPHA / R
        E = 8
        TOP_K = 2
        key = jax.random.key(seed)
        ks = jax.random.split(key, 5)
        B, S, D = (4, 256, 512)
        x = jax.random.normal(ks[0], (B, S, D), dtype=jnp.float32)
        base_W = jax.random.normal(ks[1], (D, D), dtype=jnp.float32) * 0.02
        router_W = jax.random.normal(ks[2], (E, D), dtype=jnp.float32) * 0.02
        lora_A = jax.random.normal(ks[3], (E, D, R), dtype=jnp.float32) * 0.02
        lora_B = jax.random.normal(ks[4], (E, R, D), dtype=jnp.float32) * 0.02
        return {'x': x, 'base_W': base_W, 'router_W': router_W, 'lora_A': lora_A, 'lora_B': lora_B}
    _L0_ffn_all = _L0_ffn_setup()
    _L0_ffn_in = {k: v for k, v in _L0_ffn_all.items() if k in ('base_W', 'router_W', 'lora_A', 'lora_B')}
    del _L0_ffn_all
    return {'x': x, 'ctx_4096': ctx_4096, 'g_xattn': g_xattn, 'g_ffn': g_ffn, 'L0_xattn_Wq': _L0_xattn_in['Wq'], 'L0_xattn_bq': _L0_xattn_in['bq'], 'L0_xattn_Wkv': _L0_xattn_in['Wkv'], 'L0_xattn_bkv': _L0_xattn_in['bkv'], 'L0_xattn_Wo': _L0_xattn_in['Wo'], 'L0_xattn_bo': _L0_xattn_in['bo'], 'L0_ffn_base_W': _L0_ffn_in['base_W'], 'L0_ffn_router_W': _L0_ffn_in['router_W'], 'L0_ffn_lora_A': _L0_ffn_in['lora_A'], 'L0_ffn_lora_B': _L0_ffn_in['lora_B']}

def reference(x, ctx_4096, g_xattn, g_ffn, L0_xattn_Wq, L0_xattn_bq, L0_xattn_Wkv, L0_xattn_bkv, L0_xattn_Wo, L0_xattn_bo, L0_ffn_base_W, L0_ffn_router_W, L0_ffn_lora_A, L0_ffn_lora_B):
    import jax
    import jax.numpy as jnp

    def _L0_xattn_ref(query, kv, Wq, bq, Wkv, bkv, Wo, bo):
        import jax, jax.numpy as jnp
        import numpy as np
        HID = 512
        NHEAD = 32
        NKV = 8
        HDIM = 128
        G = NHEAD // NKV
        B, L, _ = query.shape
        Lk = kv.shape[1]
        scale = jnp.asarray(1.0 / np.sqrt(HDIM), query.dtype)
        q = (query @ Wq + bq).reshape(B, L, NKV, G, HDIM)
        k_, v_ = jnp.split(kv @ Wkv + bkv, 2, axis=-1)
        k = k_.reshape(B, Lk, NKV, HDIM)
        v = v_.reshape(B, Lk, NKV, HDIM)
        scores = jnp.einsum('blkgd,bmkd->bkglm', q, k) * scale
        attn = jax.nn.softmax(scores, axis=-1)
        o = jnp.einsum('bkglm,bmkd->blkgd', attn, v).reshape(B, L, NHEAD * HDIM)
        return o @ Wo + bo

    def _L0_ffn_ref(x, base_W, router_W, lora_A, lora_B):
        import jax, jax.numpy as jnp
        import numpy as np
        R = 16
        ALPHA = 32
        SCALING = ALPHA / R
        E = 8
        TOP_K = 2
        base = jnp.einsum('bsd,od->bso', x, base_W)
        logits = jnp.einsum('bsd,ed->bse', x, router_W)
        probs = jax.nn.softmax(logits.astype(jnp.float32), axis=-1)
        top_vals, top_idx = jax.lax.top_k(probs, TOP_K)
        rw = top_vals / jnp.sum(top_vals, axis=-1, keepdims=True)
        w_dense = jnp.sum(jax.nn.one_hot(top_idx, E, dtype=rw.dtype) * rw[..., None], axis=-2).astype(x.dtype)
        mid = jnp.einsum('bsd,edr->bser', x, lora_A)
        mid = mid * w_dense[..., None]
        inc = jnp.einsum('bser,erd->bsd', mid, lora_B)
        return base + inc * SCALING
    x = x + jnp.tanh(g_xattn[0]) * _L0_xattn_ref(_layernorm(x, axis=-1), ctx_4096, L0_xattn_Wq, L0_xattn_bq, L0_xattn_Wkv, L0_xattn_bkv, L0_xattn_Wo, L0_xattn_bo)
    x = x + jnp.tanh(g_ffn[0]) * _L0_ffn_ref(_layernorm(x, axis=-1), L0_ffn_base_W, L0_ffn_router_W, L0_ffn_lora_A, L0_ffn_lora_B)
    return x

_drawn_inputs = setup_inputs


def setup_inputs(seed=0):
    import zlib

    import numpy as np

    out = dict(_drawn_inputs(seed))
    spreads = {'L0_xattn_bq': (0.0, 0.8), 'L0_xattn_bkv': (0.0, 0.1), 'L0_xattn_bo': (0.0, 0.1)}
    factors = {'L0_xattn_Wq': 3.668}
    for name, (base, spread) in spreads.items():
        noise = np.random.default_rng([zlib.crc32(name.encode()), seed]).standard_normal(out[name].shape)
        drawn = base * np.exp(spread * noise) if base else spread * noise
        out[name] = jnp.asarray(drawn.astype(out[name].dtype))
    for name, factor in factors.items():
        out[name] = (out[name] * factor).astype(out[name].dtype)
    return out
```

```python
import concourse.bass as bass
from concourse import mybir
from contextlib import ExitStack


class Count:

    def __init__(self, h):
        self.h = h
        self.n = 0

    def post(self, by=1):
        self.n += by
        return self.n


def gated_block(nc: bass.Bass, x, ctxT, gx, gf, wq, bq, wk, wv, bkv, wo, bo, bw, rw, la, lb, scr_r, scr_x, out):
    F32 = mybir.dt.float32
    F32R = mybir.dt.float32r
    ALU = mybir.AluOpType
    ACT = mybir.ActivationFunctionType
    X = mybir.AxisListType.X

    B, LQ, D, LK = 4, 256, 512, 1601
    KT = D // 128
    LKP = LK + 1
    NT = (LK + 127) // 128
    TAIL = LK - 128 * (NT - 1)
    CH = [(0, 402), (402, 400), (802, 400), (1202, 400)]
    OFF = (2048 - LKP) // 4 * 2
    SC = [(max(0, 512 * c - OFF), min(LKP, 512 * (c + 1) - OFF)) for c in range(4)]
    HALF = SC[1][1]
    NU = 16
    SCALE = 1.0 / float(128.0 ** 0.5)
    EPS = 1e-5
    E = 8
    NQ = B * LQ // 128

    queues = {n: [] for n in ("sync", "scalar", "vector", "tensor", "gpsimd")}
    waited = {}

    def do(eng, fn, post=None, by=1):
        if post is None:
            queues[eng].append(fn)
            return None
        v = post.post(by)
        queues[eng].append(lambda e: fn(e).then_inc(post.h, by))
        return v

    def need(eng, count, v):
        if v is None or v <= 0 or waited.get((eng, id(count)), 0) >= v:
            return
        waited[(eng, id(count))] = v
        queues[eng].append(lambda e: e.wait_ge(count.h, v))

    with ExitStack() as ctx:
        def sb(name, shape, dt, c=ctx):
            return c.enter_context(nc.sbuf_tensor(name, shape, dt))

        def sem(name):
            return Count(ctx.enter_context(nc.semaphore(name)))

        psS = ctx.enter_context(nc.psum_tensor("psS", [128, 2048], F32))
        psW = ctx.enter_context(nc.psum_tensor("psW", [128, 4, 512], F32))

        pth = sb("pth", [128, NT, 512], F32R)
        ptl = sb("ptl", [128, NT, 512], F32R)
        p_sb = sb("p_sb", [128, 2, LK], F32)
        kh = sb("kh", [128, LKP], F32R)
        kl = sb("kl", [128, LKP], F32R)
        vt = sb("vt", [128, LKP], F32)
        vh = sb("vh", [128, NT, 128], F32R)
        vl = sb("vl", [128, NT, 128], F32R)
        qh = sb("qh", [128, 512], F32R)
        ql = sb("ql", [128, 512], F32R)
        on = sb("on", [128, 512], F32)
        oh = sb("oh", [128, 512], F32R)
        ol = sb("ol", [128, 512], F32R)
        wqh = sb("wqh", [128, KT, 256], F32R)
        wql = sb("wql", [128, KT, 256], F32R)
        wkh = sb("wkh", [128, KT, 128], F32R)
        wkl = sb("wkl", [128, KT, 128], F32R)
        wvh = sb("wvh", [128, KT, 128], F32R)
        wvl = sb("wvl", [128, KT, 128], F32R)
        woh = sb("woh", [128, 2, 512], F32R)
        wol = sb("wol", [128, 2, 512], F32R)
        xth = sb("xth", [128, KT, 256], F32R)
        xtl = sb("xtl", [128, KT, 256], F32R)
        stg = sb("stg", [128, 2, 1024], F32)
        acc = sb("acc", [128, 2, 512], F32)
        rbc = sb("rbc", [128, 512], F32)
        bo_sb = sb("bo_sb", [128, 512], F32)
        ident = sb("ident", [128, 128], F32)
        bq_sb = sb("bq_sb", [128, 32], F32)
        bkv_sb = sb("bkv_sb", [128, 16], F32)
        tg = sb("tg", [128, 2], F32)
        st6 = sb("st6", [128, NQ, 6], F32)
        mv = sb("mv", [128, NQ, 2], F32)
        ve = sb("ve", [128, NQ], F32)
        sd = sb("sd", [128, NQ], F32)
        t1 = sb("t1", [128, NQ], F32)
        t2 = sb("t2", [128, NQ], F32)
        rstd = sb("rstd", [128, NQ], F32)
        mx = sb("mx", [128, 2, 4], F32)
        nm = sb("nm", [128, 2], F32)
        nb = sb("nb", [128, 2], F32)
        sums = sb("sums", [128, 2, 4, 2], F32)
        ssum = sb("ssum", [128, 2, 4], F32)
        rinv = sb("rinv", [128, 2, 4], F32)

        with ExitStack() as c2:
            ch = sb("ch", [128, KT, LKP], F32R, c2)
            cl = sb("cl", [128, KT, LKP], F32R, c2)
        bw_sb = sb("bw_sb", [128, KT, 512], F32)
        la_sb = sb("la_sb", [128, KT, 136], F32)
        lb_sb = sb("lb_sb", [128, 512], F32)
        x1 = sb("x1", [128, NQ, 512], F32)
        hn = sb("hn", [128, 2, 512], F32)
        hT = sb("hT", [128, 2, KT, 128], F32)
        mid = sb("mid", [128, NQ, 128], F32)
        midT = sb("midT", [128, 2, 128], F32)
        rt = sb("rt", [128, 10, NQ, E], F32)
        rs = sb("rs", [128, 8, NQ], F32)
        rev = sb("rev", [128, E], F32)

        s_w = sem("s_w")
        s_f = sem("s_f")
        s_h = sem("s_h")
        s_s = sem("s_s")
        s_nb = sem("s_nb")
        s_e = sem("s_e")
        s_d = sem("s_d")
        s_oh = sem("s_oh")
        s_ol = sem("s_ol")
        s_r = sem("s_r")
        s_pl = sem("s_pl")
        s_ph = sem("s_ph")
        s_stg = [sem("s_stg0"), sem("s_stg1")]
        s_rw = sem("s_rw")
        s_rr = sem("s_rr")
        s_c = sem("s_c")
        s_tg = sem("s_tg")
        s_id = sem("s_id")
        s_sq = sem("s_sq")
        s_acc = sem("s_acc")
        s_ac = sem("s_ac")
        s_st = sem("s_st")
        s_x1 = sem("s_x1")
        s_fw = sem("s_fw")
        s_ex = sem("s_ex")
        s_y = sem("s_y")
        s_out = sem("s_out")
        block = ctx.enter_context(nc.Block())

        def f32(ap):
            return ap.bitcast(F32)

        def dve(fn):
            need("vector", s_d, do("vector", fn, s_d))

        do("sync", lambda e: e.dma_start(bq_sb[:, :], bq), s_c, 16)
        do("sync", lambda e: e.dma_start(bkv_sb[:, :], bkv), s_c, 16)
        do("sync", lambda e: e.dma_start(tg[:, 0:1], gx.partition_broadcast(128)), s_c, 16)
        consts = do("sync", lambda e: e.dma_start(tg[:, 1:2], gf.partition_broadcast(128)), s_c, 16)
        need("gpsimd", s_id, do("gpsimd", lambda e: e.memset(ident[:, :], 0.0), s_id))
        made_id = do("gpsimd", lambda e: e.affine_select(
            out=ident[:, :], in_=ident[:, :], compare_op=ALU.not_equal, fill=1.0, base=0,
            pattern=[[-1, 128]], channel_multiplier=1), s_id)
        need("scalar", s_c, consts)
        made_tg = do("scalar", lambda e: e.activation(tg[:, :], tg[:, :], ACT.Tanh), s_tg)
        need("vector", s_c, consts)
        need("vector", s_tg, made_tg)
        padded = do("vector", lambda e: e.memset(f32(ch[:, :, LK:LKP]), 0.0), s_d)
        padded = do("vector", lambda e: e.memset(f32(cl[:, :, LK:LKP]), 0.0), s_d)

        slots = {"n": 0, 0: [], 1: []}

        def stage(src, n):
            s = slots["n"] % 2
            slots["n"] += 1
            for count, v in slots[s]:
                need("sync", count, v)
            dst = stg[:, s, 0:n]
            if len(src.shape) == 3:
                dst = dst.rearrange("p (a c) -> p a c", a=src.shape[1])
            v = do("sync", lambda e: e.dma_start(dst, src), s_stg[s], 16)
            return s, dst, s_stg[s], v

        def free_slot(s, *after):
            slots[s] = list(after)

        def split(src, n, hi, lo, after, early=False):
            s, raw, c, v = stage(src, n)
            if early:
                need("scalar", c, v)
                v = do("scalar", lambda e: e.activation(hi, raw, ACT.Copy), s_ph)
                need("vector", s_ph, v)
                v = do("vector", lambda e: e.tensor_tensor(lo, raw, f32(hi), ALU.subtract), s_d)
                free_slot(s, (s_d, v))
                return s_d, v
            need("gpsimd", c, v)
            for count, w in after:
                need("gpsimd", count, w)
            need("gpsimd", s_pl, do("gpsimd", lambda e: e.tensor_scalar(hi, raw, 1.0, 0.0, ALU.mult, ALU.add), s_pl))
            v = do("gpsimd", lambda e: e.tensor_tensor(lo, raw, f32(hi), ALU.subtract), s_pl)
            free_slot(s, (s_pl, v))
            return s_pl, v

        jobs = {"n": 0}

        def job():
            n = jobs["n"]
            jobs["n"] += 1
            need("tensor", s_f, n - 3)
            return n, psW[:, n % 4, :]

        def matmuls(mms, post):
            for k, (o, l, r) in enumerate(mms):
                last = k == len(mms) - 1
                f = (lambda e, o=o, l=l, r=r, a=(k == 0), z=last: e.matmul(o, l, r, start=a, stop=z))
                if last and post is not None:
                    return do("tensor", f, post)
                do("tensor", f)

        def three(o, lh, ll, rh, rl):
            return [(o, lh, rl), (o, lh, rh), (o, ll, rh)]

        def filled(n):
            assert s_w.n == n + 1
            return n + 1

        def emptied(n):
            assert s_f.n == n + 1

        def stats(i, src):
            dve(lambda e: e.bn_stats(st6[:, i, :], src))
            dve(lambda e: e.bn_aggr(mv[:, i, :], st6[:, i, :]))

        def rsqrt_all():
            dve(lambda e: e.tensor_scalar(ve[:, :], mv[:, :, 1], EPS, None, ALU.add))
            need("scalar", s_d, s_d.n)
            need("vector", s_sq, do("scalar", lambda e: e.activation(sd[:, :], ve[:, :], ACT.Sqrt), s_sq))
            dve(lambda e: e.reciprocal(rstd[:, :], sd[:, :]))
            dve(lambda e: e.tensor_tensor(t1[:, :], rstd[:, :], rstd[:, :], ALU.mult))
            dve(lambda e: e.tensor_tensor(t2[:, :], t1[:, :], ve[:, :], ALU.mult))
            dve(lambda e: e.tensor_scalar(t1[:, :], t2[:, :], -0.5, 1.5, ALU.mult, ALU.add))
            dve(lambda e: e.tensor_tensor(rstd[:, :], rstd[:, :], t1[:, :], ALU.mult))

        def row_stats():
            for b in range(B):
                s, raw, c, v = stage(x[:, 2 * b:2 * b + 2, :], 1024)
                need("vector", c, v)
                for t in range(2):
                    stats(2 * b + t, raw[:, t, :])
                free_slot(s, (s_d, s_d.n))
            rsqrt_all()

        ctx_ready = {}
        w_ready = {"q": None, "k": None, "v": None, "o": None}
        last_use = {"q": 0, "k": 0, "v": 0, "o": 0, "ctx": 0}

        def load_ctx(b, ks):
            for k in ks:
                for lo, n in ((0, 801), (801, 800)):
                    ctx_ready[b] = split(ctxT[b, :, k, lo:lo + n], n, ch[:, k, lo:lo + n], cl[:, k, lo:lo + n],
                                         [(s_w, last_use["ctx"])], b == 0)

        def load_wq(u):
            w_ready["q"] = split(wq[u], 1024, wqh[:, :, :].rearrange("p k n -> p (k n)"),
                                 wql[:, :, :].rearrange("p k n -> p (k n)"), [(s_w, last_use["q"])], last_use["q"] == 0)

        def load_wk(kv):
            w_ready["k"] = split(wk[kv], 512, wkh[:, :, :].rearrange("p k n -> p (k n)"),
                                 wkl[:, :, :].rearrange("p k n -> p (k n)"), [(s_w, last_use["k"])], last_use["k"] == 0)

        def load_wv(kv):
            w_ready["v"] = split(wv[kv], 512, wvh[:, :, :].rearrange("p k n -> p (k n)"),
                                 wvl[:, :, :].rearrange("p k n -> p (k n)"), [(s_w, last_use["v"])], last_use["v"] == 0)

        def load_wo(u):
            w_ready["o"] = split(wo[u], 1024, woh[:, :, :].rearrange("p k n -> p (k n)"),
                                 wol[:, :, :].rearrange("p k n -> p (k n)"), [(s_w, last_use["o"])], last_use["o"] == 0)

        xt_ready = {}

        def x_hat(b):
            s, raw, c, v = stage(x[:, 2 * b:2 * b + 2, :], 1024)
            need("vector", c, v)
            for t in range(2):
                i = 2 * b + t
                do("vector", lambda e, t=t, i=i: e.tensor_scalar(
                    raw[:, t, :], raw[:, t, :], mv[:, i, 0:1], rstd[:, i:i + 1], ALU.subtract, ALU.mult), s_d)
            need("tensor", s_d, s_d.n)
            need("tensor", s_id, made_id)
            for t in range(2):
                n, bank = job()
                for k in range(KT):
                    do("tensor", lambda e, k=k, t=t, bank=bank: e.transpose(
                        bank[:, k * 128:(k + 1) * 128], raw[:, t, k * 128:(k + 1) * 128], ident[:, :]),
                       s_w if k == KT - 1 else None)
                v = filled(n)
                src = bank.rearrange("p (k c) -> p k c", k=KT)
                hi, lo = (a[:, :, t * 128:(t + 1) * 128] for a in (xth, xtl))
                need("scalar", s_w, v)
                need("vector", s_h, do("scalar", lambda e, hi=hi, src=src: e.activation(hi, src, ACT.Copy), s_h))
                do("vector", lambda e, hi=hi, lo=lo, src=src: e.tensor_tensor(lo, src, f32(hi), ALU.subtract), s_f)
                emptied(n)
            free_slot(s, (s_w, s_w.n))
            xt_ready[b] = s_f.n

        acc_raw = {}

        def start_acc(b):
            need("sync", s_st, 16 * b)
            acc_raw[b] = do("sync", lambda e: e.dma_start(acc[:, :, :], x[:, 2 * b:2 * b + 2, :]), s_acc, 16)

        def add_bo(b):
            need("vector", s_acc, acc_raw[b])
            need("vector", s_c, bo_loaded)
            for t in range(2):
                do("vector", lambda e, t=t: e.scalar_tensor_tensor(
                    acc[:, t, :], bo_sb[:, :], tg[:, 0:1], acc[:, t, :], ALU.mult, ALU.add), s_ac)

        k_ready = {}
        q_ready = {}
        v_ready = {}

        def proj_k(b, kv):
            need("tensor", *ctx_ready[b])
            need("tensor", *w_ready["k"])
            need("tensor", s_d, padded)
            need("scalar", s_c, consts)
            for c, (lo, w) in enumerate(CH):
                n, bank = job()
                mms = []
                for k in range(KT):
                    mms += three(bank[:, 0:w], wkh[:, k, :], wkl[:, k, :], ch[:, k, lo:lo + w], cl[:, k, lo:lo + w])
                matmuls(mms, s_w)
                need("scalar", s_w, filled(n))
                bias = bkv_sb[:, kv:kv + 1]
                hi, src = kh[:, lo:lo + w], bank[:, 0:w]
                need("vector", s_h, do("scalar", lambda e, hi=hi, src=src, bias=bias: e.activation(
                    hi, src, ACT.Identity, bias=bias), s_h))
                do("vector", lambda e, hi=hi, lo_=kl[:, lo:lo + w], src=src, bias=bias: e.scalar_tensor_tensor(
                    lo_, src, bias, f32(hi), ALU.add, ALU.subtract), s_f)
                emptied(n)
                k_ready[c] = n + 1
            last_use["k"] = s_w.n
            last_use["ctx"] = s_w.n

        vt_read = {"w": 0, "f": 0}

        def proj_vt(b, kv, chunks):
            need("tensor", *ctx_ready[b])
            need("tensor", *w_ready["v"])
            for c in chunks:
                lo, w = CH[c]
                n, bank = job()
                mms = []
                for k in range(KT):
                    mms += three(bank[:, 0:w], wvh[:, k, :], wvl[:, k, :], ch[:, k, lo:lo + w], cl[:, k, lo:lo + w])
                matmuls(mms, s_w)
                need("vector", s_w, filled(n))
                bias = bkv_sb[:, 8 + kv:9 + kv]
                do("vector", lambda e, d=vt[:, lo:lo + w], src=bank[:, 0:w], bias=bias: e.tensor_scalar(
                    d, src, bias, None, ALU.add), s_f)
                emptied(n)
            vt_read["f"] = s_f.n
            last_use["v"] = s_w.n
            last_use["ctx"] = s_w.n

        def turn(src_of, hi_of, lo_of):
            for g in range(0, NT, 4):
                ts = range(g, min(g + 4, NT))
                n, bank = job()
                rows = 128
                for t in ts:
                    rows = min(128, LK - 128 * t)
                    do("tensor", lambda e, t=t, g=g, rows=rows, bank=bank: e.transpose(
                        bank[0:rows, (t - g) * 128:(t - g + 1) * 128], src_of(t, rows), ident[:, :]),
                       s_w if t == ts[-1] else None)
                v = filled(n)
                m = len(ts)
                src = bank[0:rows, 0:128 * m].rearrange("p (t c) -> p t c", t=m)
                hi, lo = hi_of(rows, g, m), lo_of(rows, g, m)
                need("scalar", s_w, v)
                hv = do("scalar", lambda e, hi=hi, src=src: e.activation(hi, src, ACT.Copy), s_h)
                need("vector", s_h, hv)
                do("vector", lambda e, hi=hi, lo=lo, src=src: e.tensor_tensor(lo, src, f32(hi), ALU.subtract), s_f)
                emptied(n)

        def turn_v():
            need("tensor", s_f, vt_read["f"])
            turn(lambda t, rows: vt[:, 128 * t:128 * t + rows],
                 lambda rows, g, m: vh[0:rows, g:g + m, :], lambda rows, g, m: vl[0:rows, g:g + m, :])
            vt_read["w"] = s_w.n
            v_ready["f"] = s_f.n

        def proj_q(b, u):
            need("tensor", *w_ready["q"])
            need("tensor", s_f, xt_ready[b])
            n, bank = job()
            for h in range(2):
                mms = []
                for k in range(KT):
                    cs = slice(h * 128, (h + 1) * 128)
                    mms += three(bank[:, h * 256:(h + 1) * 256], wqh[:, k, cs], wql[:, k, cs], xth[:, k, :], xtl[:, k, :])
                matmuls(mms, s_w if h == 1 else None)
            need("scalar", s_w, filled(n))
            for h in range(2):
                hd = 2 * u + h
                hi, src = qh[:, h * 256:(h + 1) * 256], bank[:, h * 256:(h + 1) * 256]
                hv = do("scalar", lambda e, hi=hi, src=src, hd=hd: e.activation(
                    hi, src, ACT.Identity, bias=bq_sb[:, hd:hd + 1]), s_h)
            need("vector", s_h, hv)
            for h in range(2):
                hd = 2 * u + h
                hi, lo, src = (a[:, h * 256:(h + 1) * 256] for a in (qh, ql, bank))
                do("vector", lambda e, hi=hi, lo=lo, src=src, hd=hd: e.scalar_tensor_tensor(
                    lo, src, bq_sb[:, hd:hd + 1], f32(hi), ALU.add, ALU.subtract), s_f if h == 1 else None)
            emptied(n)
            q_ready["f"] = s_f.n
            last_use["q"] = s_w.n

        e_done = {}
        t_done = {}

        def scores(i):
            j, par = i % 4, i % 2
            need("tensor", s_f, q_ready["f"])
            qs = slice(j * 128, (j + 1) * 128)
            need("tensor", s_f, max(k_ready.values()))
            for c, (lo, hi) in enumerate(SC):
                if i:
                    need("tensor", s_e, e_done[i - 1][c // 2])
                sv = matmuls(three(psS[:, OFF + lo:OFF + hi], qh[:, qs], ql[:, qs], kh[:, lo:hi], kl[:, lo:hi]), s_s)
                need("vector", s_s, sv)
                hi = min(hi, LK)
                do("vector", lambda e, c=c, lo=lo, hi=hi: e.tensor_reduce(
                    mx[:, par, c:c + 1], psS[:, OFF + lo:OFF + hi], X, ALU.max), s_d)
            need("vector", s_d, s_d.n)
            dve(lambda e: e.tensor_reduce(nm[:, par:par + 1], mx[:, par, :], X, ALU.max, negate=True))
            v = do("vector", lambda e: e.tensor_scalar(nb[:, par:par + 1], nm[:, par:par + 1], SCALE, None, ALU.mult), s_nb)
            need("scalar", s_nb, v)
            need("scalar", s_w, t_done.get(i - 2))
            up = (i // 4) % 2
            if i >= 8:
                need("scalar", s_r, i // 4 - 1)
            e_done[i] = []
            for c, (lo, hi) in enumerate(((0, HALF), (HALF, LK))):
                e_done[i].append(do("scalar", lambda e, c=c, lo=lo, hi=hi: e.activation(
                    p_sb[:, par, lo:hi], psS[:, OFF + lo:OFF + hi], ACT.Exp, bias=nb[:, par:par + 1], scale=SCALE,
                    accum_out=sums[:, up, j, c:c + 1]), s_e))

        def turn_p(i):
            j, par = i % 4, i % 2
            cs = slice(j * 128, (j + 1) * 128)
            need("tensor", s_e, e_done[i][1])
            turn(lambda t, rows: p_sb[:, par, 128 * t:128 * t + rows],
                 lambda rows, g, m: pth[0:rows, g:g + m, cs], lambda rows, g, m: ptl[0:rows, g:g + m, cs])
            t_done[i] = s_w.n
            return s_f.n

        def inverse_sums(U):
            up = U % 2
            need("vector", s_e, e_done[4 * U + 3][1])
            if U >= 2:
                need("vector", s_rw, 16 * (U - 1))
            dve(lambda e: e.tensor_tensor(ssum[:, up, :], sums[:, up, :, 0], sums[:, up, :, 1], ALU.add))
            v = do("vector", lambda e: e.reciprocal(rinv[:, up, :], ssum[:, up, :]), s_r)
            need("sync", s_r, v)
            if U >= 2:
                need("sync", s_rr, 16 * (U - 1))
            v = do("sync", lambda e: e.dma_start(scr_r[up].rearrange("(t p) -> p t", p=128), rinv[:, up, :],
                                                 allow_slow_non_contiguous=True), s_rw, 16)
            need("sync", s_rw, v)
            if U:
                need("sync", s_f, normed[U - 1])
            do("sync", lambda e: e.dma_start(rbc[:, :], scr_r[up].partition_broadcast(128)), s_rr, 16)

        pv_job = {}
        normed = {}

        def values(U, turned):
            need("tensor", s_f, v_ready["f"])
            n, bank = job()
            k, total = 0, 3 * NT
            for t in range(NT):
                need("tensor", s_f, turned - 3 + t // 4)
                rows = min(128, LK - 128 * t)
                for a, p in ((vh, pth), (vh, ptl), (vl, pth)):
                    do("tensor", lambda e, a=a, p=p, t=t, rows=rows, k=k: e.matmul(
                        bank, a[0:rows, t, :], p[0:rows, t, :], start=(k == 0), stop=(k == total - 1)),
                       s_w if k == total - 1 else None)
                    k += 1
            pv_job[U] = (filled(n), bank, n)

        def norm_o(U):
            v, bank, n = pv_job[U]
            need("vector", s_w, v)
            need("vector", s_rr, 16 * (U + 1))
            need("vector", s_oh, U)
            need("vector", s_ol, U)
            v = do("vector", lambda e: e.tensor_tensor(on[:, :], bank, rbc[:, :], ALU.mult), s_f)
            normed[U] = v
            emptied(n)
            need("scalar", s_f, v)
            if U:
                need("scalar", s_w, last_use["o"])
            do("scalar", lambda e: e.activation(oh[:, :], on[:, :], ACT.Copy), s_oh)

        def rest_o(U):
            need("vector", s_oh, U + 1)
            if U:
                need("vector", s_w, last_use["o"])
            do("vector", lambda e: e.tensor_tensor(ol[:, :], on[:, :], f32(oh[:, :]), ALU.subtract), s_ol)

        def proj_o(U, t):
            need("tensor", *w_ready["o"])
            need("tensor", s_ol, U + 1)
            n, bank = job()
            mms = []
            for h in range(2):
                cs = slice(h * 256 + t * 128, h * 256 + (t + 1) * 128)
                mms += three(bank, oh[:, cs], ol[:, cs], woh[:, h, :], wol[:, h, :])
            matmuls(mms, s_w)
            last_use["o"] = s_w.n
            need("vector", s_w, filled(n))
            need("vector", s_ac, s_ac.n)
            need("vector", s_f, acc_at[t])
            acc_at[t] = do("vector", lambda e, t=t: e.scalar_tensor_tensor(
                acc[:, t, :], bank, tg[:, 0:1], acc[:, t, :], ALU.mult, ALU.add), s_f)
            emptied(n)

        acc_at = {0: 0, 1: 0}

        def store_acc(b):
            need("sync", s_f, max(acc_at.values()))
            do("sync", lambda e: e.dma_start(scr_x[:, 2 * b:2 * b + 2, :], acc[:, :, :]), s_st, 16)

        load_wk(0)
        load_ctx(0, range(KT))
        proj_k(0, 0)
        row_stats()
        x_hat(0)
        load_wq(0)
        load_wv(0)
        proj_q(0, 0)
        load_wk(1)
        load_wq(1)
        scores(0)
        proj_vt(0, 0, (0, 1))
        bo_loaded = do("sync", lambda e: e.dma_start(bo_sb[:, :], bo.partition_broadcast(128)), s_c, 16)
        start_acc(0)
        add_bo(0)
        load_wo(0)
        UN = B * NU
        for U in range(UN):
            b, u = divmod(U, NU)
            nb_, nu_ = divmod(U + 1, NU)
            more = U + 1 < UN
            kv = u // 2
            odd = u % 2
            nvb, nvk = divmod(8 * b + kv + 1, 8) if odd else (b, kv)
            whole = odd and kv == 6
            for j in range(3):
                i = 4 * U + j
                if j == 0 and U:
                    norm_o(U - 1)
                if not odd and j == 2:
                    turn_v()
                    if (kv, b) != (7, B - 1):
                        load_wv((kv + 1) % 8)
                scores(i + 1)
                if j == 0 and U:
                    rest_o(U - 1)
                if j == 0 and u == 1 and b:
                    add_bo(b)
                if j and U:
                    proj_o(U - 1, j - 1)
                    if j == 2:
                        if u == 0:
                            store_acc(b - 1)
                            start_acc(b)
                        load_wo(u)
                if odd and nvk and nvb < B:
                    if j < 2:
                        proj_vt(nvb, nvk, (2 * j, 2 * j + 1) if whole else (j,))
                if not odd and kv != 7 and j < 2:
                    proj_vt(b, kv, (0, 1) if kv == 0 and b and j == 0 else (2, 3) if kv == 0 and b else (j + 2,))
                if j == 2 and more:
                    proj_q(nb_, nu_)
                    if U + 2 < UN:
                        load_wq((nu_ + 1) % NU)
                    if u == 14 and b + 1 < B:
                        x_hat(b + 1)
                        load_ctx(b + 1, range(2, KT))
                turn_p(i)
            if more:
                if odd:
                    proj_k(nb_, nu_ // 2)
                    if (nu_ // 2, nb_) != (7, B - 1):
                        load_wk((nu_ // 2 + 1) % 8)
            if u == 13 and b + 1 < B:
                load_ctx(b + 1, range(2))
            turned = turn_p(4 * U + 3)
            if more:
                scores(4 * U + 4)
            inverse_sums(U)
            values(U, turned)
        norm_o(UN - 1)
        rest_o(UN - 1)
        for t in range(2):
            proj_o(UN - 1, t)
        store_acc(B - 1)

        need("sync", s_w, s_w.n)
        need("sync", s_f, s_f.n)
        need("sync", s_pl, s_pl.n)
        need("sync", s_st, s_st.n)
        do("sync", lambda e: e.dma_start(x1[:, :, :], scr_x), s_x1, 16)
        do("sync", lambda e: e.dma_start(la_sb[:, :, 0:128], la), s_fw, 16)
        do("sync", lambda e: e.dma_start(la_sb[:, :, 128:136], rw), s_fw, 16)
        do("sync", lambda e: e.dma_start(bw_sb[:, :, :], bw), s_fw, 16)
        do("sync", lambda e: e.dma_start(lb_sb[:, :], lb), s_fw, 16)
        need("gpsimd", s_w, s_w.n)
        need("gpsimd", s_f, s_f.n)
        need("gpsimd", s_pl, s_pl.n)
        need("vector", s_w, s_w.n)
        need("vector", s_pl, s_pl.n)
        need("scalar", s_w, s_w.n)
        for e_ in range(E):
            made_rev = do("gpsimd", lambda e, e_=e_: e.memset(rev[:, e_:e_ + 1], float(E - e_)), s_id)
        need("vector", s_x1, 16)
        for i in range(NQ):
            stats(i, x1[:, i, :])
        rsqrt_all()
        ht_at = {}

        def h_norm(i):
            do("vector", lambda e: e.tensor_scalar(hn[:, i % 2, :], x1[:, i, :], mv[:, i, 0:1], rstd[:, i:i + 1],
                                                   ALU.subtract, ALU.mult), s_d)
            return s_d.n

        def h_turn(i, hv, dst):
            need("tensor", s_d, hv)
            n, bank = job()
            for k in range(KT):
                do("tensor", lambda e, k=k: e.transpose(bank[:, k * 128:(k + 1) * 128],
                                                        hn[:, i % 2, k * 128:(k + 1) * 128], ident[:, :]),
                   s_w if k == KT - 1 else None)
            need("vector", s_w, filled(n))
            do("vector", lambda e: e.tensor_copy(dst, bank.rearrange("p (k c) -> p k c", k=KT)), s_f)
            emptied(n)
            return n + 1

        need("tensor", s_fw, 64)
        for i in range(NQ):
            if i >= 2:
                need("vector", s_w, ht_at[i - 2])
            hv = h_norm(i)
            r = h_turn(i, hv, hT[:, i % 2, :, :])
            need("tensor", s_f, r)
            n, bank = job()
            matmuls([(bank[:, 0:136], hT[:, i % 2, k, :], la_sb[:, k, :]) for k in range(KT)], s_w)
            ht_at[i] = filled(n)
            need("vector", s_w, ht_at[i])
            do("vector", lambda e, i=i, bank=bank: e.tensor_copy(mid[:, i, :], bank[:, 0:128]))
            do("vector", lambda e, i=i, bank=bank: e.tensor_copy(rt[:, 0, i, :], bank[:, 128:136]), s_f)
            emptied(n)
        need("vector", s_f, s_f.n)
        bc = lambda ap: ap.unsqueeze(2).to_broadcast([128, NQ, E])
        rv = rev[:, :].unsqueeze(1).to_broadcast([128, NQ, E])
        need("vector", s_id, made_rev)
        R = lambda k: rt[:, k, :, :]
        S_ = lambda k: rs[:, k, :]
        dve(lambda e: e.tensor_reduce(S_(0), R(0), X, ALU.max))
        dve(lambda e: e.tensor_tensor(R(1), R(0), bc(S_(0)), ALU.subtract))
        need("scalar", s_d, s_d.n)
        need("vector", s_ex, do("scalar", lambda e: e.activation(R(2), R(1), ACT.Exp), s_ex))
        dve(lambda e: e.tensor_reduce(S_(1), R(2), X, ALU.add))
        dve(lambda e: e.reciprocal(S_(2), S_(1)))
        dve(lambda e: e.tensor_tensor(R(3), R(2), bc(S_(2)), ALU.mult))
        dve(lambda e: e.tensor_reduce(S_(3), R(3), X, ALU.max))
        dve(lambda e: e.tensor_tensor(R(4), R(3), bc(S_(3)), ALU.is_equal))
        dve(lambda e: e.tensor_tensor(R(4), R(4), rv, ALU.mult))
        dve(lambda e: e.tensor_reduce(S_(4), R(4), X, ALU.max))
        dve(lambda e: e.tensor_tensor(R(5), rv, bc(S_(4)), ALU.is_equal))
        dve(lambda e: e.scalar_tensor_tensor(R(6), R(5), -2.0, R(3), ALU.mult, ALU.add))
        dve(lambda e: e.tensor_reduce(S_(5), R(6), X, ALU.max))
        dve(lambda e: e.tensor_tensor(R(7), R(6), bc(S_(5)), ALU.is_equal))
        dve(lambda e: e.tensor_tensor(R(7), R(7), rv, ALU.mult))
        dve(lambda e: e.tensor_reduce(S_(6), R(7), X, ALU.max))
        dve(lambda e: e.tensor_tensor(R(8), rv, bc(S_(6)), ALU.is_equal))
        dve(lambda e: e.tensor_tensor(S_(7), S_(3), S_(5), ALU.add))
        dve(lambda e: e.reciprocal(S_(7), S_(7)))
        dve(lambda e: e.tensor_tensor(R(5), R(5), bc(S_(3)), ALU.mult))
        dve(lambda e: e.tensor_tensor(R(8), R(8), bc(S_(5)), ALU.mult))
        dve(lambda e: e.tensor_tensor(R(5), R(5), R(8), ALU.add))
        dve(lambda e: e.tensor_scalar(S_(7), S_(7), 2.0, None, ALU.mult))
        dve(lambda e: e.tensor_tensor(R(9), R(5), bc(S_(7)), ALU.mult))
        y_at = {}
        for i in range(NQ):
            if i >= 2:
                need("vector", s_w, y_at[i - 2])
            hv = h_norm(i)
            do("vector", lambda e, i=i: e.tensor_tensor(
                mid[:, i, :].rearrange("p (e r) -> p e r", e=E), mid[:, i, :].rearrange("p (e r) -> p e r", e=E),
                rt[:, 9, i, :].unsqueeze(2).to_broadcast([128, E, 16]), ALU.mult), s_d)
            mvv = s_d.n
            if i >= 2:
                need("vector", s_w, y_at[i - 2])
            else:
                need("vector", s_w, ht_at[NQ - 1])
            r = h_turn(i, hv, hT[:, i % 2, :, :])
            need("tensor", s_d, mvv)
            n, bank = job()
            do("tensor", lambda e, i=i, bank=bank: e.transpose(bank[:, 0:128], mid[:, i, :], ident[:, :]), s_w)
            need("vector", s_w, filled(n))
            do("vector", lambda e, i=i, bank=bank: e.tensor_copy(midT[:, i % 2, :], bank[:, 0:128]), s_f)
            emptied(n)
            r = n + 1
            need("tensor", s_f, r)
            n, bank = job()
            mms = [(bank, hT[:, i % 2, k, :], bw_sb[:, k, :]) for k in range(KT)]
            matmuls(mms + [(bank, midT[:, i % 2, :], lb_sb[:, :])], s_w)
            y_at[i] = filled(n)
            need("vector", s_w, y_at[i])
            v = do("vector", lambda e, i=i, bank=bank: e.scalar_tensor_tensor(
                x1[:, i, :], bank, tg[:, 1:2], x1[:, i, :], ALU.mult, ALU.add), s_f)
            emptied(n)
            need("sync", s_f, v)
            do("sync", lambda e, i=i: e.dma_start(out[:, i, :], x1[:, i, :]), s_out, 16)
        need("sync", s_out, s_out.n)
        need("sync", s_rw, s_rw.n)

        @block.sync
        def _(eng):
            for f in queues["sync"]:
                f(eng)

        @block.gpsimd
        def _(eng):
            for f in queues["gpsimd"]:
                f(eng)

        @block.scalar
        def _(eng):
            for f in queues["scalar"]:
                f(eng)

        @block.vector
        def _(eng):
            for f in queues["vector"]:
                f(eng)

        @block.tensor
        def _(eng):
            for f in queues["tensor"]:
                f(eng)


def kernel(**inputs):
    import numpy as np
    import concourse.bacc as bacc
    from concourse.bass_utils import run_bass_kernel_spmd

    a = {k: np.asarray(v) for k, v in inputs.items()}
    B, LQ, D = a["x"].shape
    kt = D // 128
    wkv = a["L0_xattn_Wkv"]

    def by_column(w, n):
        c = w.shape[1] // n
        return w.reshape(kt, 128, n, c).transpose(2, 1, 0, 3).reshape(n, 128, kt * c)

    def by_row(w):
        return w.reshape(kt, 128, -1).transpose(1, 0, 2)

    E, _, R = a["L0_ffn_lora_A"].shape
    laid = {
        "x": a["x"].reshape(B * LQ // 128, 128, D).transpose(1, 0, 2),
        "ctxT": a["ctx_4096"].transpose(0, 2, 1).reshape(B, kt, 128, -1).transpose(0, 2, 1, 3),
        "gx": a["g_xattn"], "gf": a["g_ffn"],
        "wq": by_column(a["L0_xattn_Wq"], 16), "bq": a["L0_xattn_bq"].reshape(32, 128).T,
        "wk": by_column(wkv[:, :1024], 8), "wv": by_column(wkv[:, 1024:], 8),
        "bkv": a["L0_xattn_bkv"].reshape(16, 128).T,
        "wo": a["L0_xattn_Wo"].reshape(16, 2, 128, D).transpose(0, 2, 1, 3).reshape(16, 128, 2 * D),
        "bo": a["L0_xattn_bo"],
        "bw": by_row(a["L0_ffn_base_W"].T), "rw": by_row(a["L0_ffn_router_W"].T),
        "la": by_row(a["L0_ffn_lora_A"].transpose(1, 0, 2).reshape(D, E * R)),
        "lb": a["L0_ffn_lora_B"].reshape(E * R, D),
    }
    nc = bacc.Bacc("TRN2", target_bir_lowering=False, num_devices=1)
    f32 = mybir.dt.float32
    arrays, args = {}, []
    for name, v in laid.items():
        v = np.ascontiguousarray(v)
        arrays["in_" + name] = v
        args.append(nc.dram_tensor("in_" + name, v.shape, mybir.dt.from_np(v.dtype), kind="ExternalInput").ap())
    args.append(nc.dram_tensor("scr_r", (2, 512), f32, kind="Internal").ap())
    args.append(nc.dram_tensor("scr_x", (128, B * LQ // 128, D), f32, kind="Internal").ap())
    args.append(nc.dram_tensor("out_0", (128, B * LQ // 128, D), f32, kind="ExternalOutput").ap())
    gated_block(nc, *args)
    r = run_bass_kernel_spmd(nc, [arrays], core_ids=[0])
    y = r.results[0]["out_0"]
    return np.ascontiguousarray(y.transpose(1, 0, 2)).reshape(B, LQ, D)
```

```python
import concourse.bass as bass
from concourse import mybir
from contextlib import ExitStack


class Count:

    def __init__(self, h):
        self.h = h
        self.n = 0

    def post(self, by=1):
        self.n += by
        return self.n


def gated_block(nc: bass.Bass, x, ctxT, gx, gf, wq, bq, wk, wv, bkv, wo, bo, bw, rw, la, lb, scr_r, scr_x, out):
    F32 = mybir.dt.float32
    F32R = mybir.dt.float32r
    ALU = mybir.AluOpType
    ACT = mybir.ActivationFunctionType
    X = mybir.AxisListType.X

    B, LQ, D, LK = 4, 256, 512, 1601
    KT = D // 128
    LKP = LK + 1
    NT = (LK + 127) // 128
    TAIL = LK - 128 * (NT - 1)
    CH = [(0, 402), (402, 400), (802, 400), (1202, 400)]
    OFF = (2048 - LKP) // 4 * 2
    SC = [(max(0, 512 * c - OFF), min(LKP, 512 * (c + 1) - OFF)) for c in range(4)]
    HALF = SC[1][1]
    NU = 16
    PIECE = 404
    BO = 96
    SCALE = 1.0 / float(128.0 ** 0.5)
    EPS = 1e-5
    E = 8
    NQ = B * LQ // 128

    queues = {n: [] for n in ("sync", "scalar", "vector", "tensor", "gpsimd")}
    waited = {}

    def do(eng, fn, post=None, by=1):
        if post is None:
            queues[eng].append(fn)
            return None
        v = post.post(by)
        queues[eng].append(lambda e: fn(e).then_inc(post.h, by))
        return v

    def need(eng, count, v):
        if v is None or v <= 0 or waited.get((eng, id(count)), 0) >= v:
            return
        waited[(eng, id(count))] = v
        queues[eng].append(lambda e: e.wait_ge(count.h, v))

    with ExitStack() as ctx:
        def sb(name, shape, dt, c=ctx):
            return c.enter_context(nc.sbuf_tensor(name, shape, dt))

        def sem(name):
            return Count(ctx.enter_context(nc.semaphore(name)))

        psS = ctx.enter_context(nc.psum_tensor("psS", [128, 2048], F32))
        psW = ctx.enter_context(nc.psum_tensor("psW", [128, 4, 512], F32))

        with ExitStack() as c1:
            praw = sb("praw", [128, NT * 512], F32, c1)
            lraw = sb("lraw", [128, NT * 512], F32, c1)
            on = sb("on", [128, 512], F32, c1)
            xraw = sb("xraw", [128, 2, 512], F32, c1)
        pth = sb("pth", [128, NT, 512], F32R)
        ptl = sb("ptl", [128, NT, 512], F32R)
        ol = sb("ol", [128, 512], F32R)
        wvh = sb("wvh", [128, KT, 256], F32R)
        p_sb = sb("p_sb", [128, 2, LK], F32)
        kh = sb("kh", [128, LKP], F32R)
        kl = sb("kl", [128, LKP], F32R)
        vh = sb("vh", [128, NT, 256], F32R)
        vl = sb("vl", [128, NT, 256], F32R)
        qh = sb("qh", [128, 512], F32R)
        ql = sb("ql", [128, 512], F32R)
        oh = sb("oh", [128, 512], F32R)
        wqh = sb("wqh", [128, KT, 256], F32R)
        wql = sb("wql", [128, KT, 256], F32R)
        wkh = sb("wkh", [128, KT, 128], F32R)
        wkl = sb("wkl", [128, KT, 128], F32R)
        wvl = sb("wvl", [128, KT, 256], F32R)
        woh = sb("woh", [128, 2, 512], F32R)
        wol = sb("wol", [128, 2, 512], F32R)
        xth = sb("xth", [128, KT, 256], F32R)
        xtl = sb("xtl", [128, KT, 256], F32R)
        stg = sb("stg", [128, 2, PIECE], F32)
        acc = sb("acc", [128, 2, 512], F32)
        rbc = sb("rbc", [128, 512], F32)
        ident = sb("ident", [128, 128], F32)
        bq_sb = sb("bq_sb", [128, 32], F32)
        bkv_sb = sb("bkv_sb", [128, 16], F32)
        tg = sb("tg", [128, 2], F32)
        mv = sb("mv", [128, NQ, 2], F32)
        rstd = sb("rstd", [128, NQ], F32)
        rstds = sb("rstds", [128, NQ], F32)
        mx = sb("mx", [128, 2, 3], F32)
        nm = sb("nm", [128, 2], F32)
        sums = sb("sums", [128, 2, 4, 2], F32)
        ssum = sb("ssum", [128, 2, 4], F32)
        rinv = sb("rinv", [128, 2, 4], F32)

        with ExitStack() as c2:
            ch = sb("ch", [128, KT, LKP], F32R, c2)
            cl = sb("cl", [128, KT, LKP], F32R, c2)
        bw_sb = sb("bw_sb", [128, KT, 512], F32)
        la_sb = sb("la_sb", [128, KT, 136], F32)
        lb_sb = sb("lb_sb", [128, 512], F32)
        x1 = sb("x1", [128, NQ - 2, 512], F32)
        hn = sb("hn", [128, 512], F32)
        hT = sb("hT", [128, NQ, KT, 128], F32)
        mid = sb("mid", [128, NQ, 136], F32)
        midT = sb("midT", [128, 2, 128], F32)
        rt = sb("rt", [128, 9, NQ, E], F32)
        rs = sb("rs", [128, 8, NQ], F32)
        rev = sb("rev", [128, E], F32)
        steps = sb("steps", [128, 40], F32)

        s_w = sem("s_w")
        s_f = sem("s_f")
        s_h = sem("s_h")
        s_s = sem("s_s")
        s_nb = sem("s_nb")
        s_e = sem("s_e")
        s_d = sem("s_d")
        s_oh = sem("s_oh")
        s_ol = sem("s_ol")
        s_r = sem("s_r")
        s_pl = sem("s_pl")
        s_ph = sem("s_ph")
        s_stg = [sem("s_stg0"), sem("s_stg1")]
        s_rw = sem("s_rw")
        s_rr = sem("s_rr")
        s_c = sem("s_c")
        s_tg = sem("s_tg")
        s_id = sem("s_id")
        s_sq = sem("s_sq")
        s_acc = sem("s_acc")
        s_in = {k: sem("s_in_" + k) for k in ("x", "wk", "c0", "c1", "c2", "c3", "wq", "wv", "xr", "bo")}
        s_st = sem("s_st")
        s_x = sem("s_x")
        s_x1 = sem("s_x1")
        s_fw = sem("s_fw")
        s_ex = sem("s_ex")
        s_y = sem("s_y")
        s_out = sem("s_out")
        block = ctx.enter_context(nc.Block())

        def f32(ap):
            return ap.bitcast(F32)

        def dve(fn):
            need("vector", s_d, do("vector", fn, s_d))

        do("sync", lambda e: e.dma_start(bq_sb[:, :], bq), s_c, 16)
        do("sync", lambda e: e.dma_start(bkv_sb[:, :], bkv), s_c, 16)
        do("sync", lambda e: e.dma_start(tg[:, 0:1], gx.partition_broadcast(128)), s_c, 16)
        consts = do("sync", lambda e: e.dma_start(tg[:, 1:2], gf.partition_broadcast(128)), s_c, 16)
        need("gpsimd", s_id, do("gpsimd", lambda e: e.memset(ident[:, :], 0.0), s_id))
        made_id = do("gpsimd", lambda e: e.affine_select(
            out=ident[:, :], in_=ident[:, :], compare_op=ALU.not_equal, fill=1.0, base=0,
            pattern=[[-1, 128]], channel_multiplier=1), s_id)
        need("scalar", s_c, consts)
        made_tg = do("scalar", lambda e: e.activation(tg[:, :], tg[:, :], ACT.Tanh), s_tg)
        need("vector", s_c, consts)
        need("vector", s_tg, made_tg)
        dve(lambda e: e.tensor_scalar(bq_sb[:, :], bq_sb[:, :], SCALE, None, ALU.mult))
        scaled_bq = s_d.n
        padded = do("vector", lambda e: e.memset(f32(ch[:, :, LK:LKP]), 0.0), s_d)
        padded = do("vector", lambda e: e.memset(f32(cl[:, :, LK:LKP]), 0.0), s_d)

        slots = {"n": 0, 0: [], 1: []}

        def stage(src, n):
            s = slots["n"] % 2
            slots["n"] += 1
            for count, v in slots[s]:
                need("sync", count, v)
            dst = stg[:, s, 0:n]
            v = do("sync", lambda e: e.dma_start(dst, src), s_stg[s], 16)
            return s, dst, s_stg[s], v

        def free_slot(s, *after):
            slots[s] = list(after)

        def split(src, hi, lo, after):
            width = src.shape[1]
            count = -(-width // PIECE)
            step = -(-width // (2 * count)) * 2
            for a in range(0, width, step):
                z = min(width, a + step)
                s, raw, c, v = stage(src[:, a:z], z - a)
                need("gpsimd", c, v)
                for other, w in after:
                    need("gpsimd", other, w)
                need("gpsimd", s_pl, do("gpsimd", lambda e, a=a, z=z, raw=raw: e.tensor_scalar(
                    hi[:, a:z], raw, 1.0, 0.0, ALU.mult, ALU.add), s_pl))
                v = do("gpsimd", lambda e, a=a, z=z, raw=raw: e.tensor_tensor(
                    lo[:, a:z], raw, f32(hi[:, a:z]), ALU.subtract), s_pl)
                free_slot(s, (s_pl, v))
            return s_pl, v

        def split_early(raw, hi, lo, name):
            need("scalar", s_in[name], s_in[name].n)
            v = do("scalar", lambda e: e.activation(hi, raw, ACT.Copy), s_ph)
            need("vector", s_ph, v)
            return s_d, do("vector", lambda e: e.tensor_tensor(lo, raw, f32(hi), ALU.subtract), s_d)

        jobs = {"n": 0}

        def job():
            n = jobs["n"]
            jobs["n"] += 1
            need("tensor", s_f, n - 3)
            return n, psW[:, n % 4, :]

        def matmuls(mms, post):
            for k, (o, l, r) in enumerate(mms):
                last = k == len(mms) - 1
                f = (lambda e, o=o, l=l, r=r, a=(k == 0), z=last: e.matmul(o, l, r, start=a, stop=z))
                if last and post is not None:
                    return do("tensor", f, post)
                do("tensor", f)

        def three(o, lh, ll, rh, rl):
            return [(o, lh, rl), (o, lh, rh), (o, ll, rh)]

        def filled(n):
            assert s_w.n == n + 1
            return n + 1

        def emptied(n):
            assert s_f.n == n + 1

        def stats(i, src, tmp):
            st6 = tmp[:, 0:6]
            dve(lambda e: e.bn_stats(st6, src))
            dve(lambda e: e.bn_aggr(mv[:, i, :], st6))

        def inverse_dev(a, z, tmp):
            ve, sd, t1, t2 = (tmp[:, 8 * k:8 * k + 8] for k in range(1, 5))
            dve(lambda e: e.tensor_scalar(ve[:, a:z], mv[:, a:z, 1], EPS, None, ALU.add))
            need("scalar", s_d, s_d.n)
            need("vector", s_sq, do("scalar", lambda e: e.activation(sd[:, a:z], ve[:, a:z], ACT.Sqrt), s_sq))
            dve(lambda e: e.reciprocal(rstd[:, a:z], sd[:, a:z]))
            dve(lambda e: e.tensor_tensor(t1[:, a:z], rstd[:, a:z], rstd[:, a:z], ALU.mult))
            dve(lambda e: e.tensor_tensor(t2[:, a:z], t1[:, a:z], ve[:, a:z], ALU.mult))
            dve(lambda e: e.tensor_scalar(t1[:, a:z], t2[:, a:z], -0.5, 1.5, ALU.mult, ALU.add))
            dve(lambda e: e.tensor_tensor(rstd[:, a:z], rstd[:, a:z], t1[:, a:z], ALU.mult))

        def scaled_dev(a, z):
            dve(lambda e: e.tensor_scalar(rstds[:, a:z], rstd[:, a:z], SCALE, None, ALU.mult))

        ctx_ready = {}
        w_ready = {"q": None, "k": None, "v": None, "o": None}
        last_use = {"q": 0, "k": 0, "v": 0, "o": 0, "ctx": 0}

        def flat(t):
            return t[:, :, :].rearrange("p k n -> p (k n)")

        def load_ctx(b, ks):
            for k in ks:
                ctx_ready[b] = [split(ctxT[b, :, k, :], ch[:, k, :], cl[:, k, :], [(s_w, last_use["ctx"])])] * 4

        def load_wq(u):
            w_ready["q"] = split(wq[u], flat(wqh), flat(wql), [(s_w, last_use["q"])])

        def load_wk(kv):
            w_ready["k"] = split(wk[kv], flat(wkh), flat(wkl), [(s_w, last_use["k"])])

        def load_wv(p):
            w_ready["v"] = split(wv[p], flat(wvh), flat(wvl), [(s_w, max(last_use["v"], x_hat_at.get("w", 0)))])

        def load_wo(u):
            w_ready["o"] = split(wo[u], flat(woh), flat(wol), [(s_w, last_use["o"])])

        xt_ready = {}
        x_hat_at = {}

        def x_hat_load(b):
            need("sync", s_w, last_use["v"])
            do("sync", lambda e: e.dma_start(xraw[:, :, :], x[:, 2 * b:2 * b + 2, :]), s_x, 16)

        def x_hat(b, t, raw, count, v):
            i = 2 * b + t
            need("vector", count, v)
            do("vector", lambda e: e.tensor_scalar(
                raw, raw, mv[:, i, 0:1], rstds[:, i:i + 1], ALU.subtract, ALU.mult), s_d)
            need("tensor", s_d, s_d.n)
            need("tensor", s_id, made_id)
            n, bank = job()
            for k in range(KT):
                do("tensor", lambda e, k=k: e.transpose(
                    bank[:, k * 128:(k + 1) * 128], raw[:, k * 128:(k + 1) * 128], ident[:, :]),
                   s_w if k == KT - 1 else None)
            v = x_hat_at["w"] = filled(n)
            src = bank.rearrange("p (k c) -> p k c", k=KT)
            hi, lo = (a[:, :, t * 128:(t + 1) * 128] for a in (xth, xtl))
            need("scalar", s_w, v)
            need("vector", s_h, do("scalar", lambda e: e.activation(hi, src, ACT.Copy), s_h))
            do("vector", lambda e: e.tensor_tensor(lo, src, f32(hi), ALU.subtract), s_f)
            emptied(n)
            xt_ready[b] = s_f.n

        acc_ready = {}

        def start_acc(b):
            need("sync", s_st, 16 * b)
            acc_ready[b] = do("sync", lambda e: e.dma_start(acc[:, :, :], x[:, 2 * b:2 * b + 2, :]), s_acc, 16)

        k_ready = {}
        q_ready = {}
        v_ready = {}

        def proj_k(b, kv, chunks=range(4)):
            need("tensor", *w_ready["k"])
            need("tensor", s_d, padded)
            need("scalar", s_c, consts)
            for c in chunks:
                lo, w = CH[c]
                need("tensor", *ctx_ready[b][c])
                n, bank = job()
                mms = []
                for k in range(KT):
                    mms += three(bank[:, 0:w], wkh[:, k, :], wkl[:, k, :], ch[:, k, lo:lo + w], cl[:, k, lo:lo + w])
                matmuls(mms, s_w)
                need("scalar", s_w, filled(n))
                bias = bkv_sb[:, kv:kv + 1]
                hi, src = kh[:, lo:lo + w], bank[:, 0:w]
                need("vector", s_h, do("scalar", lambda e, hi=hi, src=src, bias=bias: e.activation(
                    hi, src, ACT.Identity, bias=bias), s_h))
                do("vector", lambda e, hi=hi, lo_=kl[:, lo:lo + w], src=src, bias=bias: e.scalar_tensor_tensor(
                    lo_, src, bias, f32(hi), ALU.add, ALU.subtract), s_f)
                emptied(n)
                k_ready[c] = n + 1
            last_use["k"] = s_w.n
            last_use["ctx"] = s_w.n

        def proj_v(b, p, groups):
            need("tensor", *ctx_ready[b][3])
            need("tensor", *w_ready["v"])
            for g in groups:
                ts = range(2 * g, min(2 * g + 2, NT))
                n, bank = job()
                for t in ts:
                    rows = min(128, LK - 128 * t)
                    mms = []
                    for k in range(KT):
                        ps = slice(128 * t, 128 * t + rows)
                        mms += three(bank[0:rows, (t - 2 * g) * 256:(t - 2 * g + 1) * 256], ch[:, k, ps], cl[:, k, ps],
                                     wvh[:, k, :], wvl[:, k, :])
                    matmuls(mms, s_w if t == ts[-1] else None)
                m = len(ts)
                src = bank[0:rows, 0:256 * m].rearrange("p (t c) -> p t c", t=m)
                hi, lo = (a[0:rows, 2 * g:2 * g + m, :] for a in (vh, vl))
                need("scalar", s_w, filled(n))
                need("vector", s_h, do("scalar", lambda e, hi=hi, src=src: e.activation(hi, src, ACT.Copy), s_h))
                do("vector", lambda e, hi=hi, lo=lo, src=src: e.tensor_tensor(lo, src, f32(hi), ALU.subtract), s_f)
                emptied(n)
            v_ready["f"] = s_f.n
            last_use["v"] = s_w.n
            last_use["ctx"] = s_w.n

        def turn(src_of, hi_of, lo_of):
            for g, z in ((NT - 1, NT), (0, 4), (4, 8), (8, 12)):
                ts = range(g, z)
                n, bank = job()
                rows = 128
                for t in ts:
                    rows = min(128, LK - 128 * t)
                    do("tensor", lambda e, t=t, g=g, rows=rows, bank=bank: e.transpose(
                        bank[0:rows, (t - g) * 128:(t - g + 1) * 128], src_of(t, rows), ident[:, :]),
                       s_w if t == ts[-1] else None)
                v = filled(n)
                m = len(ts)
                src = bank[0:rows, 0:128 * m].rearrange("p (t c) -> p t c", t=m)
                hi, lo = hi_of(rows, g, m), lo_of(rows, g, m)
                need("scalar", s_w, v)
                hv = do("scalar", lambda e, hi=hi, src=src: e.activation(hi, src, ACT.Copy), s_h)
                need("vector", s_h, hv)
                do("vector", lambda e, hi=hi, lo=lo, src=src: e.tensor_tensor(lo, src, f32(hi), ALU.subtract), s_f)
                emptied(n)

        def proj_q(b, u):
            need("tensor", *w_ready["q"])
            need("tensor", s_f, xt_ready[b])
            n, bank = job()
            for h in range(2):
                mms = []
                for k in range(KT):
                    cs = slice(h * 128, (h + 1) * 128)
                    mms += three(bank[:, h * 256:(h + 1) * 256], wqh[:, k, cs], wql[:, k, cs], xth[:, k, :], xtl[:, k, :])
                matmuls(mms, s_w if h == 1 else None)
            need("scalar", s_w, filled(n))
            need("scalar", s_d, scaled_bq)
            for h in range(2):
                hd = 2 * u + h
                hi, src = qh[:, h * 256:(h + 1) * 256], bank[:, h * 256:(h + 1) * 256]
                hv = do("scalar", lambda e, hi=hi, src=src, hd=hd: e.activation(
                    hi, src, ACT.Identity, bias=bq_sb[:, hd:hd + 1]), s_h)
            need("vector", s_h, hv)
            for h in range(2):
                hd = 2 * u + h
                hi, lo, src = (a[:, h * 256:(h + 1) * 256] for a in (qh, ql, bank))
                do("vector", lambda e, hi=hi, lo=lo, src=src, hd=hd: e.scalar_tensor_tensor(
                    lo, src, bq_sb[:, hd:hd + 1], f32(hi), ALU.add, ALU.subtract), s_f if h == 1 else None)
            emptied(n)
            q_ready["f"] = s_f.n
            last_use["q"] = s_w.n

        e_done = {}
        t_done = {}

        def scores(i, between=None):
            j, par = i % 4, i % 2
            need("tensor", s_f, q_ready["f"])
            qs = slice(j * 128, (j + 1) * 128)
            need("tensor", s_f, max(k_ready.values()))
            for c, (lo, hi) in enumerate(SC):
                if i:
                    need("tensor", s_e, e_done[i - 1][c // 2])
                sv = matmuls(three(psS[:, OFF + lo:OFF + hi], qh[:, qs], ql[:, qs], kh[:, lo:hi], kl[:, lo:hi]), s_s)
                if c:
                    need("vector", s_s, sv)
                    lo, hi = 0 if c == 1 else lo, min(hi, LK)
                    v = do("vector", lambda e, c=c, lo=lo, hi=hi: e.tensor_reduce(
                        mx[:, par, c - 1:c], psS[:, OFF + lo:OFF + hi], X, ALU.max), s_d)
                    if between and c == 1:
                        between()
            need("vector", s_d, v)
            m_done[i] = do("vector", lambda e: e.tensor_reduce(nm[:, par:par + 1], mx[:, par, :], X, ALU.max, negate=True),
                           s_nb)

        m_done = {}

        def exps(i):
            j, par, up = i % 4, i % 2, (i // 4) % 2
            need("scalar", s_nb, m_done[i])
            need("scalar", s_w, t_done.get(i - 2))
            if i >= 8:
                need("scalar", s_r, i // 4 - 1)
            e_done[i] = []
            for c, (lo, hi) in enumerate(((0, HALF), (HALF, LK))):
                e_done[i].append(do("scalar", lambda e, c=c, lo=lo, hi=hi: e.activation(
                    p_sb[:, par, lo:hi], psS[:, OFF + lo:OFF + hi], ACT.Exp, bias=nm[:, par:par + 1],
                    accum_out=sums[:, up, j, c:c + 1]), s_e))

        def turn_p(i):
            j, par = i % 4, i % 2
            cs = slice(j * 128, (j + 1) * 128)
            need("tensor", s_e, e_done[i][1])
            turn(lambda t, rows: p_sb[:, par, 128 * t:128 * t + rows],
                 lambda rows, g, m: pth[0:rows, g:g + m, cs], lambda rows, g, m: ptl[0:rows, g:g + m, cs])
            t_done[i] = s_w.n
            return s_f.n

        def inverse_sums(U):
            up = U % 2
            need("vector", s_e, e_done[4 * U + 3][1])
            if U >= 2:
                need("vector", s_rw, 16 * (U - 1))
            dve(lambda e: e.tensor_tensor(ssum[:, up, :], sums[:, up, :, 0], sums[:, up, :, 1], ALU.add))
            v = do("vector", lambda e: e.reciprocal(rinv[:, up, :], ssum[:, up, :]), s_r)
            need("sync", s_r, v)
            if U >= 2:
                need("sync", s_rr, 16 * (U - 1))
            v = do("sync", lambda e: e.dma_start(scr_r[up].rearrange("(t p) -> p t", p=128), rinv[:, up, :],
                                                 allow_slow_non_contiguous=True), s_rw, 16)
            need("sync", s_rw, v)
            if U:
                need("sync", s_f, normed[U - 1])
            do("sync", lambda e: e.dma_start(rbc[:, :], scr_r[up].partition_broadcast(128)), s_rr, 16)

        pv_job = {}
        normed = {}

        def values(U, turned):
            need("tensor", s_f, v_ready["f"])
            hs = slice(128 * (U // 2 % 2), 128 * (U // 2 % 2) + 128)
            n, bank = job()
            k, total = 0, 3 * NT
            for t in range(NT):
                need("tensor", s_f, turned - 2 + t // 4 if t < NT - 1 else turned - 3)
                rows = min(128, LK - 128 * t)
                for a, p in ((vh, pth), (vh, ptl), (vl, pth)):
                    do("tensor", lambda e, a=a, p=p, t=t, rows=rows, k=k: e.matmul(
                        bank, a[0:rows, t, hs], p[0:rows, t, :], start=(k == 0), stop=(k == total - 1)),
                       s_w if k == total - 1 else None)
                    k += 1
            pv_job[U] = (filled(n), bank, n)

        def norm_o(U):
            v, bank, n = pv_job[U]
            need("vector", s_w, v)
            need("vector", s_rr, 16 * (U + 1))
            need("vector", s_oh, U)
            need("vector", s_ol, U)
            if U:
                need("vector", s_w, last_use["o"])
                need("scalar", s_w, last_use["o"])
            v = do("vector", lambda e: e.tensor_tensor(on[:, :], bank, rbc[:, :], ALU.mult), s_f)
            normed[U] = v
            emptied(n)
            need("scalar", s_f, v)
            bias = bkv_sb[:, 8 + U % NU // 2:9 + U % NU // 2]
            do("scalar", lambda e: e.activation(oh[:, :], on[:, :], ACT.Identity, bias=bias), s_oh)

        def rest_o(U):
            need("vector", s_oh, U + 1)
            bias = bkv_sb[:, 8 + U % NU // 2:9 + U % NU // 2]
            do("vector", lambda e: e.scalar_tensor_tensor(
                ol[:, :], on[:, :], bias, f32(oh[:, :]), ALU.add, ALU.subtract), s_ol)

        def proj_o(U, t):
            need("tensor", *w_ready["o"])
            need("tensor", s_ol, U + 1)
            n, bank = job()
            mms = []
            for h in range(2):
                cs = slice(h * 256 + t * 128, h * 256 + (t + 1) * 128)
                mms += three(bank, oh[:, cs], ol[:, cs], woh[:, h, :], wol[:, h, :])
            if U % NU == 0:
                need("tensor", s_d, bo_split)
                mms += [(bank, one_row, bo_lo), (bank, one_row, bo_hi)]
            matmuls(mms, s_w)
            last_use["o"] = s_w.n
            need("vector", s_w, filled(n))
            need("vector", s_acc, acc_ready[U // NU])
            need("vector", s_f, acc_at[t])
            acc_at[t] = do("vector", lambda e, t=t: e.scalar_tensor_tensor(
                acc[:, t, :], bank, tg[:, 0:1], acc[:, t, :], ALU.mult, ALU.add), s_f)
            emptied(n)

        acc_at = {0: 0, 1: 0}

        def store_acc(b):
            need("sync", s_f, max(acc_at.values()))
            do("sync", lambda e: e.dma_start(scr_x[:, 2 * b:2 * b + 2, :], acc[:, :, :]), s_st, 16)

        made = {}

        def ffn_load():
            need("sync", s_w, last_use["ctx"])
            need("sync", s_st, 16 * (B - 1))
            do("sync", lambda e: e.dma_start(x1[:, :, :], scr_x[:, 0:NQ - 2, :]), s_x1, 16)
            do("sync", lambda e: e.dma_start(la_sb[:, :, 0:128], la), s_fw, 16)
            do("sync", lambda e: e.dma_start(la_sb[:, :, 128:136], rw), s_fw, 16)
            do("sync", lambda e: e.dma_start(bw_sb[:, :, :], bw), s_fw, 16)
            do("sync", lambda e: e.dma_start(lb_sb[:, :], lb), s_fw, 16)
            need("gpsimd", s_w, last_use["ctx"])
            for e_ in range(E):
                made["rev"] = do("gpsimd", lambda e, e_=e_: e.memset(rev[:, e_:e_ + 1], float(E - e_)), s_id)

        def tile_of(i):
            return x1[:, i, :] if i < NQ - 2 else acc[:, i - (NQ - 2), :]

        turned_h = {}

        def ffn_turn(i):
            need("vector", s_w, turned_h.get("w"))
            hv = do("vector", lambda e: e.tensor_scalar(hn[:, :], tile_of(i), mv[:, i, 0:1], rstd[:, i:i + 1],
                                                        ALU.subtract, ALU.mult), s_d)
            need("tensor", s_d, hv)
            n, bank = job()
            for k in range(KT):
                do("tensor", lambda e, k=k: e.transpose(bank[:, k * 128:(k + 1) * 128], hn[:, k * 128:(k + 1) * 128],
                                                        ident[:, :]), s_w if k == KT - 1 else None)
            turned_h["w"] = filled(n)
            need("vector", s_w, filled(n))
            turned_h[i] = do("vector", lambda e: e.tensor_copy(hT[:, i, :, :], bank.rearrange("p (k c) -> p k c", k=KT)),
                             s_f)
            emptied(n)

        mid_at = {}

        def ffn_mid(i):
            need("tensor", s_fw, 64)
            need("tensor", s_f, turned_h[i])
            n, bank = job()
            matmuls([(bank[:, 0:136], hT[:, i, k, :], la_sb[:, k, :]) for k in range(KT)], s_w)
            need("vector", s_w, filled(n))
            mid_at[i] = do("vector", lambda e: e.tensor_copy(mid[:, i, :], bank[:, 0:136]), s_f)
            emptied(n)

        def route(a, z):
            shape = [128, z - a, E]
            bc = lambda ap: ap.unsqueeze(2).to_broadcast(shape)
            rv = rev[:, :].unsqueeze(1).to_broadcast(shape)
            R = lambda k: rt[:, k - 1, a:z, :] if k else mid[:, a:z, 128:136]
            S_ = lambda k: rs[:, k, a:z]
            need("vector", s_f, mid_at[z - 1])
            need("vector", s_id, made["rev"])
            dve(lambda e: e.tensor_reduce(S_(0), R(0), X, ALU.max))
            dve(lambda e: e.tensor_tensor(R(1), R(0), bc(S_(0)), ALU.subtract))
            need("scalar", s_d, s_d.n)
            need("vector", s_ex, do("scalar", lambda e: e.activation(R(2), R(1), ACT.Exp), s_ex))
            dve(lambda e: e.tensor_reduce(S_(1), R(2), X, ALU.add))
            dve(lambda e: e.reciprocal(S_(2), S_(1)))
            dve(lambda e: e.tensor_tensor(R(3), R(2), bc(S_(2)), ALU.mult))
            dve(lambda e: e.tensor_reduce(S_(3), R(3), X, ALU.max))
            dve(lambda e: e.tensor_tensor(R(4), R(3), bc(S_(3)), ALU.is_equal))
            dve(lambda e: e.tensor_tensor(R(4), R(4), rv, ALU.mult))
            dve(lambda e: e.tensor_reduce(S_(4), R(4), X, ALU.max))
            dve(lambda e: e.tensor_tensor(R(5), rv, bc(S_(4)), ALU.is_equal))
            dve(lambda e: e.scalar_tensor_tensor(R(6), R(5), -2.0, R(3), ALU.mult, ALU.add))
            dve(lambda e: e.tensor_reduce(S_(5), R(6), X, ALU.max))
            dve(lambda e: e.tensor_tensor(R(7), R(6), bc(S_(5)), ALU.is_equal))
            dve(lambda e: e.tensor_tensor(R(7), R(7), rv, ALU.mult))
            dve(lambda e: e.tensor_reduce(S_(6), R(7), X, ALU.max))
            dve(lambda e: e.tensor_tensor(R(8), rv, bc(S_(6)), ALU.is_equal))
            dve(lambda e: e.tensor_tensor(S_(7), S_(3), S_(5), ALU.add))
            dve(lambda e: e.reciprocal(S_(7), S_(7)))
            dve(lambda e: e.tensor_tensor(R(5), R(5), bc(S_(3)), ALU.mult))
            dve(lambda e: e.tensor_tensor(R(8), R(8), bc(S_(5)), ALU.mult))
            dve(lambda e: e.tensor_tensor(R(5), R(5), R(8), ALU.add))
            dve(lambda e: e.tensor_scalar(S_(7), S_(7), 2.0, None, ALU.mult))
            dve(lambda e: e.tensor_tensor(R(9), R(5), bc(S_(7)), ALU.mult))

        gated = {}
        y_at = {}

        def ffn_gate(i):
            need("vector", s_f, mid_at[i])
            v = do("vector", lambda e: e.tensor_tensor(
                mid[:, i, 0:128].rearrange("p (e r) -> p e r", e=E), mid[:, i, 0:128].rearrange("p (e r) -> p e r", e=E),
                rt[:, 8, i, :].unsqueeze(2).to_broadcast([128, E, 16]), ALU.mult), s_d)
            need("tensor", s_d, v)
            n, bank = job()
            do("tensor", lambda e: e.transpose(bank[:, 0:128], mid[:, i, 0:128], ident[:, :]), s_w)
            need("vector", s_w, filled(n))
            need("vector", s_w, y_at.get(i - 2))
            gated[i] = do("vector", lambda e: e.tensor_copy(midT[:, i % 2, :], bank[:, 0:128]), s_f)
            emptied(n)

        def ffn_y(i):
            need("tensor", s_f, gated[i])
            n, bank = job()
            mms = [(bank, hT[:, i, k, :], bw_sb[:, k, :]) for k in range(KT)]
            y_at[i] = matmuls(mms + [(bank, midT[:, i % 2, :], lb_sb[:, :])], s_w)
            need("vector", s_w, filled(n))
            v = do("vector", lambda e: e.scalar_tensor_tensor(
                tile_of(i), bank, tg[:, 1:2], tile_of(i), ALU.mult, ALU.add), s_f)
            emptied(n)
            need("sync", s_f, v)
            do("sync", lambda e: e.dma_start(out[:, i, :], tile_of(i)), s_out, 16)

        def fetch(name, dst, src):
            do("sync", lambda e: e.dma_start(dst, src), s_in[name], 16)
            return dst

        x_raw = fetch("x", lraw[:, 0:1024].rearrange("p (t c) -> p t c", t=2), x[:, 0:2, :])
        wk_raw = fetch("wk", lraw[:, 1024:1536], wk[0])
        c_raw = []
        for c, (lo, w) in enumerate(CH):
            w = min(w, LK - lo)
            c_raw.append(fetch("c%d" % c, praw[:, KT * lo:KT * (lo + w)].rearrange("p (k c) -> p k c", k=KT),
                               ctxT[0, :, :, lo:lo + w]))
        wq_raw = fetch("wq", lraw[:, 1536:2560], wq[0])
        wv_raw = fetch("wv", lraw[:, 5632:6656], wv[0])
        xr_raw = fetch("xr", lraw[:, 2560:5632].rearrange("p (t c) -> p t c", t=6), x[:, 2:8, :])
        fetch("bo", rbc[BO:BO + 1, :], bo.unsqueeze(0))
        start_acc(0)

        w_ready["k"] = split_early(wk_raw, flat(wkh), flat(wkl), "wk")
        need("vector", s_in["x"], 16)
        for t in range(2):
            stats(t, x_raw[:, t, :], on)
        inverse_dev(0, 2, on)
        scaled_dev(0, 2)
        for t in range(2):
            x_hat(0, t, x_raw[:, t, :], s_in["x"], 16)
        ctx_ready[0] = []
        for c, (lo, w) in enumerate(CH):
            w = min(w, LK - lo)
            ctx_ready[0].append(split_early(c_raw[c], ch[:, :, lo:lo + w], cl[:, :, lo:lo + w], "c%d" % c))
            if c:
                proj_k(0, 0, [c - 1])
        w_ready["q"] = split_early(wq_raw, flat(wqh), flat(wql), "wq")
        proj_k(0, 0, [3])
        proj_q(0, 0)
        load_wk(1)
        load_wq(1)
        scores(0)
        w_ready["v"] = split_early(wv_raw, flat(wvh), flat(wvl), "wv")
        exps(0)
        proj_v(0, 0, range(4))
        need("vector", s_in["xr"], 16)
        for i in range(2, NQ):
            stats(i, xr_raw[:, i - 2, :], on)
        inverse_dev(2, NQ, on)
        scaled_dev(2, NQ)
        bo_hi, bo_lo, one_row = pth[BO:BO + 1, NT - 1, :], ptl[BO:BO + 1, NT - 1, :], vh[BO:BO + 1, NT - 1, 0:128]
        split_early(rbc[BO:BO + 1, :], bo_hi, bo_lo, "bo")
        bo_split = do("vector", lambda e: e.tensor_scalar(one_row, rbc[BO:BO + 1, 0:128], 0.0, 1.0, ALU.mult, ALU.add), s_d)
        load_wo(0)
        UN = B * NU
        for U in range(UN):
            b, u = divmod(U, NU)
            nb_, nu_ = divmod(U + 1, NU)
            more = U + 1 < UN
            kind, pair = u % 4, u // 4
            turning = u == 14 and b + 1 < B
            for j in range(3):
                i = 4 * U + j
                if j == 0 and U:
                    norm_o(U - 1)
                scores(i + 1, (lambda: rest_o(U - 1)) if j == 0 and U else None)
                turn_p(i)
                exps(i + 1)
                if j < 2 and U:
                    proj_o(U - 1, j)
                    if j == 1 and u == 0:
                        store_acc(b - 1)
                        start_acc(b)
                    if j == 1:
                        load_wo(u)
                if kind == 0:
                    proj_v(b, pair, (4 + j,) if U == 0 else (2 * j, 2 * j + 1))
                if j == 2 and more:
                    proj_q(nb_, nu_)
                    if turning:
                        x_hat(b + 1, 0, xraw[:, 0, :], s_x, 16 * (b + 1))
                    if U + 2 < UN:
                        load_wq((nu_ + 1) % NU)
                if not more:
                    if j:
                        ffn_mid(j - 1)
                    ffn_turn(j)
            if kind == 0 and U:
                proj_v(b, pair, (6,))
            if kind % 2 and more:
                proj_k(nb_, nu_ // 2)
            if not more:
                ffn_mid(2)
                ffn_turn(3)
            turned = turn_p(4 * U + 3)
            if more:
                scores(4 * U + 4)
                exps(4 * U + 4)
            if turning:
                x_hat(b + 1, 1, xraw[:, 1, :], s_x, 16 * (b + 1))
            inverse_sums(U)
            if kind == 0 and pair < 3:
                load_wv(pair + 1)
            if u == 12 and b + 1 < B:
                x_hat_load(b + 1)
            if kind % 2 and more and (nu_ // 2, nb_) != (7, B - 1):
                load_wk((nu_ // 2 + 1) % 8)
            if u == 13 and b + 1 < B:
                load_ctx(b + 1, range(3))
            if turning:
                load_ctx(b + 1, range(3, KT))
                load_wv(0)
            if u == 13 and b == B - 1:
                ffn_load()
            if U == UN - 2:
                need("vector", s_x1, 16)
                for i in range(NQ - 2):
                    stats(i, x1[:, i, :], steps)
                inverse_dev(0, NQ - 2, steps)
            if not more:
                ffn_mid(3)
                for i in (4, 5):
                    ffn_turn(i)
                    ffn_mid(i)
            values(U, turned)
        route(0, NQ - 2)
        norm_o(UN - 1)
        ffn_gate(0)
        rest_o(UN - 1)
        ffn_y(0)
        for t in range(2):
            proj_o(UN - 1, t)
        ffn_gate(1)
        need("vector", s_f, max(acc_at.values()))
        for i in (6, 7):
            stats(i, acc[:, i - 6, :], steps)
        inverse_dev(6, 8, steps)
        ffn_y(1)
        ffn_gate(2)
        ffn_turn(6)
        ffn_y(2)
        ffn_gate(3)
        ffn_mid(6)
        ffn_turn(7)
        ffn_y(3)
        ffn_gate(4)
        ffn_mid(7)
        ffn_y(4)
        ffn_gate(5)
        route(6, 8)
        ffn_y(5)
        ffn_gate(6)
        ffn_gate(7)
        ffn_y(6)
        ffn_y(7)
        need("sync", s_out, s_out.n)
        need("sync", s_st, s_st.n)
        need("sync", s_rw, s_rw.n)

        @block.sync
        def _(eng):
            for f in queues["sync"]:
                f(eng)

        @block.gpsimd
        def _(eng):
            for f in queues["gpsimd"]:
                f(eng)

        @block.scalar
        def _(eng):
            for f in queues["scalar"]:
                f(eng)

        @block.vector
        def _(eng):
            for f in queues["vector"]:
                f(eng)

        @block.tensor
        def _(eng):
            for f in queues["tensor"]:
                f(eng)


def kernel(**inputs):
    import numpy as np
    import concourse.bacc as bacc
    from concourse.bass_utils import run_bass_kernel_spmd

    a = {k: np.asarray(v) for k, v in inputs.items()}
    B, LQ, D = a["x"].shape
    kt = D // 128
    wkv = a["L0_xattn_Wkv"]

    def by_column(w, n):
        c = w.shape[1] // n
        return w.reshape(kt, 128, n, c).transpose(2, 1, 0, 3).reshape(n, 128, kt * c)

    def by_row(w):
        return w.reshape(kt, 128, -1).transpose(1, 0, 2)

    E, _, R = a["L0_ffn_lora_A"].shape
    laid = {
        "x": a["x"].reshape(B * LQ // 128, 128, D).transpose(1, 0, 2),
        "ctxT": a["ctx_4096"].transpose(0, 2, 1).reshape(B, kt, 128, -1).transpose(0, 2, 1, 3),
        "gx": a["g_xattn"], "gf": a["g_ffn"],
        "wq": by_column(a["L0_xattn_Wq"], 16), "bq": a["L0_xattn_bq"].reshape(32, 128).T,
        "wk": by_column(wkv[:, :1024], 8), "wv": by_column(wkv[:, 1024:], 4),
        "bkv": a["L0_xattn_bkv"].reshape(16, 128).T,
        "wo": a["L0_xattn_Wo"].reshape(16, 2, 128, D).transpose(0, 2, 1, 3).reshape(16, 128, 2 * D),
        "bo": a["L0_xattn_bo"],
        "bw": by_row(a["L0_ffn_base_W"].T), "rw": by_row(a["L0_ffn_router_W"].T),
        "la": by_row(a["L0_ffn_lora_A"].transpose(1, 0, 2).reshape(D, E * R)),
        "lb": a["L0_ffn_lora_B"].reshape(E * R, D),
    }
    nc = bacc.Bacc("TRN2", target_bir_lowering=False, num_devices=1)
    f32 = mybir.dt.float32
    arrays, args = {}, []
    for name, v in laid.items():
        v = np.ascontiguousarray(v)
        arrays["in_" + name] = v
        args.append(nc.dram_tensor("in_" + name, v.shape, mybir.dt.from_np(v.dtype), kind="ExternalInput").ap())
    args.append(nc.dram_tensor("scr_r", (2, 512), f32, kind="Internal").ap())
    args.append(nc.dram_tensor("scr_x", (128, B * LQ // 128, D), f32, kind="Internal").ap())
    args.append(nc.dram_tensor("out_0", (128, B * LQ // 128, D), f32, kind="ExternalOutput").ap())
    gated_block(nc, *args)
    r = run_bass_kernel_spmd(nc, [arrays], core_ids=[0])
    y = r.results[0]["out_0"]
    return np.ascontiguousarray(y.transpose(1, 0, 2)).reshape(B, LQ, D)
```

```python
import concourse.bass as bass
from concourse import mybir
from contextlib import ExitStack


class Count:

    def __init__(self, h):
        self.h = h
        self.n = 0

    def post(self, by=1):
        self.n += by
        return self.n


def gated_block(nc: bass.Bass, x, ctxT, gx, gf, wq, bq, wk, wv, bkv, wo, bo, bw, rw, la, lb, scr_r, scr_x, out):
    F32 = mybir.dt.float32
    F32R = mybir.dt.float32r
    ALU = mybir.AluOpType
    ACT = mybir.ActivationFunctionType
    X = mybir.AxisListType.X

    B, LQ, D, LK = 4, 256, 512, 1601
    KT = D // 128
    LKP = LK + 1
    NT = (LK + 127) // 128
    CH = [(0, 402), (402, 400), (802, 400), (1202, 400)]
    OFF = (2048 - LKP) // 4 * 2
    SC = [(max(0, 512 * c - OFF), min(LKP, 512 * (c + 1) - OFF)) for c in range(4)]
    HALF = SC[1][1]
    NU = 16
    PIECE = 404
    BO = 96
    SCALE = 1.0 / float(128.0 ** 0.5)
    EPS = 1e-5
    E = 8
    NQ = B * LQ // 128

    queues = {n: [] for n in ("sync", "scalar", "vector", "tensor", "gpsimd")}
    waited = {}

    def do(eng, fn, post=None, by=1):
        if post is None:
            queues[eng].append(fn)
            return None
        v = post.post(by)
        queues[eng].append(lambda e: fn(e).then_inc(post.h, by))
        return v

    def need(eng, count, v):
        if v is None or v <= 0 or waited.get((eng, id(count)), 0) >= v:
            return
        waited[(eng, id(count))] = v
        queues[eng].append(lambda e: e.wait_ge(count.h, v))

    with ExitStack() as ctx:
        def sb(name, shape, dt, c=ctx):
            return c.enter_context(nc.sbuf_tensor(name, shape, dt))

        def sem(name):
            return Count(ctx.enter_context(nc.semaphore(name)))

        psS = ctx.enter_context(nc.psum_tensor("psS", [128, 2048], F32))
        psW = ctx.enter_context(nc.psum_tensor("psW", [128, 4, 512], F32))

        with ExitStack() as c1:
            praw = sb("praw", [128, NT * 512], F32, c1)
            lraw = sb("lraw", [128, NT * 512], F32, c1)
            on = sb("on", [128, 512], F32, c1)
            xraw = sb("xraw", [128, 2, 512], F32, c1)
        pth = sb("pth", [128, NT, 512], F32R)
        ptl = sb("ptl", [128, NT, 512], F32R)
        ol = sb("ol", [128, 512], F32R)
        wvh = sb("wvh", [128, KT, 256], F32R)
        p_sb = sb("p_sb", [128, 2, LK], F32)
        kh = sb("kh", [128, LKP], F32R)
        kl = sb("kl", [128, LKP], F32R)
        vh = sb("vh", [128, NT, 256], F32R)
        vl = sb("vl", [128, NT, 256], F32R)
        qh = sb("qh", [128, 512], F32R)
        ql = sb("ql", [128, 512], F32R)
        oh = sb("oh", [128, 512], F32R)
        wqh = sb("wqh", [128, KT, 256], F32R)
        wql = sb("wql", [128, KT, 256], F32R)
        wkh = sb("wkh", [128, KT, 128], F32R)
        wkl = sb("wkl", [128, KT, 128], F32R)
        wvl = sb("wvl", [128, KT, 256], F32R)
        woh = sb("woh", [128, 2, 512], F32R)
        wol = sb("wol", [128, 2, 512], F32R)
        xth = sb("xth", [128, KT, 256], F32R)
        xtl = sb("xtl", [128, KT, 256], F32R)
        stg = sb("stg", [128, 2, PIECE], F32)
        acc = sb("acc", [128, 2, 512], F32)
        rbc = sb("rbc", [128, 512], F32)
        ident = sb("ident", [128, 128], F32)
        bq_sb = sb("bq_sb", [128, 32], F32)
        bkv_sb = sb("bkv_sb", [128, 16], F32)
        tg = sb("tg", [128, 2], F32)
        mv = sb("mv", [128, NQ, 2], F32)
        rstd = sb("rstd", [128, NQ], F32)
        rstds = sb("rstds", [128, NQ], F32)
        mx = sb("mx", [128, 2, 3], F32)
        nm = sb("nm", [128, 2], F32)
        sums = sb("sums", [128, 2, 4, 2], F32)
        ssum = sb("ssum", [128, 2, 4], F32)
        rinv = sb("rinv", [128, 2, 4], F32)

        with ExitStack() as c2:
            ch = sb("ch", [128, KT, LKP], F32R, c2)
            cl = sb("cl", [128, KT, LKP], F32R, c2)
        bw_sb = sb("bw_sb", [128, KT, 512], F32)
        la_sb = sb("la_sb", [128, KT, 136], F32)
        lb_sb = sb("lb_sb", [128, 512], F32)
        x1 = sb("x1", [128, NQ - 2, 512], F32)
        hn = sb("hn", [128, 512], F32)
        hT = sb("hT", [128, NQ, KT, 128], F32)
        mid = sb("mid", [128, NQ, 136], F32)
        midT = sb("midT", [128, 2, 128], F32)
        rt = sb("rt", [128, 9, NQ, E], F32)
        rs = sb("rs", [128, 8, NQ], F32)
        rev = sb("rev", [128, E], F32)
        steps = sb("steps", [128, 40], F32)

        s_w = sem("s_w")
        s_f = sem("s_f")
        s_h = sem("s_h")
        s_s = sem("s_s")
        s_nb = sem("s_nb")
        s_e = sem("s_e")
        s_d = sem("s_d")
        s_oh = sem("s_oh")
        s_ol = sem("s_ol")
        s_r = sem("s_r")
        s_pl = sem("s_pl")
        s_ph = sem("s_ph")
        s_stg = [sem("s_stg0"), sem("s_stg1")]
        s_rw = sem("s_rw")
        s_rr = sem("s_rr")
        s_c = sem("s_c")
        s_tg = sem("s_tg")
        s_id = sem("s_id")
        s_sq = sem("s_sq")
        s_acc = sem("s_acc")
        s_in = {k: sem("s_in_" + k) for k in ("x", "wk", "c0", "c1", "c2", "c3", "xr", "bo")}
        s_st = sem("s_st")
        s_x = sem("s_x")
        s_x1 = sem("s_x1")
        s_fw = sem("s_fw")
        s_ex = sem("s_ex")
        s_y = sem("s_y")
        s_out = sem("s_out")
        block = ctx.enter_context(nc.Block())

        def f32(ap):
            return ap.bitcast(F32)

        def dve(fn):
            need("vector", s_d, do("vector", fn, s_d))

        do("sync", lambda e: e.dma_start(bq_sb[:, :], bq), s_c, 16)
        do("sync", lambda e: e.dma_start(bkv_sb[:, :], bkv), s_c, 16)
        do("sync", lambda e: e.dma_start(tg[:, 0:1], gx.partition_broadcast(128)), s_c, 16)
        consts = do("sync", lambda e: e.dma_start(tg[:, 1:2], gf.partition_broadcast(128)), s_c, 16)
        need("gpsimd", s_id, do("gpsimd", lambda e: e.memset(ident[:, :], 0.0), s_id))
        made_id = do("gpsimd", lambda e: e.affine_select(
            out=ident[:, :], in_=ident[:, :], compare_op=ALU.not_equal, fill=1.0, base=0,
            pattern=[[-1, 128]], channel_multiplier=1), s_id)
        need("scalar", s_c, consts)
        made_tg = do("scalar", lambda e: e.activation(tg[:, :], tg[:, :], ACT.Tanh), s_tg)
        need("vector", s_c, consts)
        need("vector", s_tg, made_tg)
        dve(lambda e: e.tensor_scalar(bq_sb[:, :], bq_sb[:, :], SCALE, None, ALU.mult))
        scaled_bq = s_d.n
        padded = do("vector", lambda e: e.memset(f32(ch[:, :, LK:LKP]), 0.0), s_d)
        padded = do("vector", lambda e: e.memset(f32(cl[:, :, LK:LKP]), 0.0), s_d)

        slots = {"n": 0, 0: [], 1: []}

        def stage(src, n):
            s = slots["n"] % 2
            slots["n"] += 1
            for count, v in slots[s]:
                need("sync", count, v)
            dst = stg[:, s, 0:n]
            v = do("sync", lambda e: e.dma_start(dst, src), s_stg[s], 16)
            return s, dst, s_stg[s], v

        def free_slot(s, *after):
            slots[s] = list(after)

        def split(src, hi, lo, after):
            width = src.shape[1]
            count = -(-width // PIECE)
            step = -(-width // (2 * count)) * 2
            for a in range(0, width, step):
                z = min(width, a + step)
                s, raw, c, v = stage(src[:, a:z], z - a)
                need("gpsimd", c, v)
                for other, w in after:
                    need("gpsimd", other, w)
                need("gpsimd", s_pl, do("gpsimd", lambda e, a=a, z=z, raw=raw: e.tensor_scalar(
                    hi[:, a:z], raw, 1.0, 0.0, ALU.mult, ALU.add), s_pl))
                v = do("gpsimd", lambda e, a=a, z=z, raw=raw: e.tensor_tensor(
                    lo[:, a:z], raw, f32(hi[:, a:z]), ALU.subtract), s_pl)
                free_slot(s, (s_pl, v))
            return s_pl, v

        def split_early(raw, hi, lo, name):
            need("scalar", s_in[name], s_in[name].n)
            v = do("scalar", lambda e: e.activation(hi, raw, ACT.Copy), s_ph)
            need("vector", s_ph, v)
            return s_d, do("vector", lambda e: e.tensor_tensor(lo, raw, f32(hi), ALU.subtract), s_d)

        banks = [(k, None) for k in range(4)]

        def job():
            n, v = banks.pop(0)
            need("tensor", s_f, v)
            return n, psW[:, n, :]

        def matmuls(mms, post):
            for k, (o, l, r) in enumerate(mms):
                last = k == len(mms) - 1
                f = (lambda e, o=o, l=l, r=r, a=(k == 0), z=last: e.matmul(o, l, r, start=a, stop=z))
                if last and post is not None:
                    return do("tensor", f, post)
                do("tensor", f)

        def three(o, lh, ll, rh, rl):
            return [(o, lh, rl), (o, lh, rh), (o, ll, rh)]

        def filled(n):
            return s_w.n

        def emptied(n):
            banks.append((n, s_f.n))

        def stats(i, src, tmp):
            st6 = tmp[:, 0:6]
            dve(lambda e: e.bn_stats(st6, src))
            dve(lambda e: e.bn_aggr(mv[:, i, :], st6))

        def inverse_dev(a, z, tmp):
            ve, sd, t1, t2 = (tmp[:, 8 * k:8 * k + 8] for k in range(1, 5))
            dve(lambda e: e.tensor_scalar(ve[:, a:z], mv[:, a:z, 1], EPS, None, ALU.add))
            need("scalar", s_d, s_d.n)
            need("vector", s_sq, do("scalar", lambda e: e.activation(sd[:, a:z], ve[:, a:z], ACT.Sqrt), s_sq))
            dve(lambda e: e.reciprocal(rstd[:, a:z], sd[:, a:z]))
            dve(lambda e: e.tensor_tensor(t1[:, a:z], rstd[:, a:z], rstd[:, a:z], ALU.mult))
            dve(lambda e: e.tensor_tensor(t2[:, a:z], t1[:, a:z], ve[:, a:z], ALU.mult))
            dve(lambda e: e.tensor_scalar(t1[:, a:z], t2[:, a:z], -0.5, 1.5, ALU.mult, ALU.add))
            dve(lambda e: e.tensor_tensor(rstd[:, a:z], rstd[:, a:z], t1[:, a:z], ALU.mult))

        def scaled_dev(a, z):
            dve(lambda e: e.tensor_scalar(rstds[:, a:z], rstd[:, a:z], SCALE, None, ALU.mult))

        ctx_ready = {}
        w_ready = {"q": None, "k": None, "v": None, "o": None}
        last_use = {"q": 0, "k": 0, "v": 0, "o": 0, "ctx": 0}

        def flat(t):
            return t[:, :, :].rearrange("p k n -> p (k n)")

        def load_ctx(b, ks):
            for k in ks:
                ctx_ready[b] = [split(ctxT[b, :, k, :], ch[:, k, :], cl[:, k, :], [(s_w, last_use["ctx"])])] * 4

        def load_wq(u):
            w_ready["q"] = split(wq[u], flat(wqh), flat(wql), [(s_w, last_use["q"])])

        def load_wk(kv):
            w_ready["k"] = split(wk[kv], flat(wkh), flat(wkl), [(s_w, last_use["k"])])

        def load_wv(p):
            w_ready["v"] = split(wv[p], flat(wvh), flat(wvl), [(s_w, max(last_use["v"], x_hat_at.get("w", 0)))])

        def load_wo(u):
            w_ready["o"] = split(wo[u], flat(woh), flat(wol), [(s_w, last_use["o"])])

        xt_ready = {}
        x_hat_at = {}

        def x_hat_load(b):
            need("sync", s_w, last_use["v"])
            do("sync", lambda e: e.dma_start(xraw[:, :, :], x[:, 2 * b:2 * b + 2, :]), s_x, 16)

        x_normed = {}

        def x_norm(i, raw, count, v):
            need("vector", count, v)
            x_normed[i] = do("vector", lambda e: e.tensor_scalar(
                raw, raw, mv[:, i, 0:1], rstds[:, i:i + 1], ALU.subtract, ALU.mult), s_d)

        def x_hat(b, t, raw):
            need("tensor", s_d, x_normed[2 * b + t])
            need("tensor", s_id, made_id)
            n, bank = job()
            for k in range(KT):
                do("tensor", lambda e, k=k: e.transpose(
                    bank[:, k * 128:(k + 1) * 128], raw[:, k * 128:(k + 1) * 128], ident[:, :]),
                   s_w if k == KT - 1 else None)
            v = x_hat_at["w"] = filled(n)
            src = bank.rearrange("p (k c) -> p k c", k=KT)
            hi, lo = (a[:, :, t * 128:(t + 1) * 128] for a in (xth, xtl))
            need("scalar", s_w, v)
            need("vector", s_h, do("scalar", lambda e: e.activation(hi, src, ACT.Copy), s_h))
            do("vector", lambda e: e.tensor_tensor(lo, src, f32(hi), ALU.subtract), s_f)
            emptied(n)
            xt_ready[b] = s_f.n

        acc_ready = {}

        def start_acc(b):
            need("sync", s_st, 16 * b)
            acc_ready[b] = do("sync", lambda e: e.dma_start(acc[:, :, :], x[:, 2 * b:2 * b + 2, :]), s_acc, 16)

        k_ready = {}
        q_ready = {}
        v_ready = {}

        def proj_k(b, kv, chunks=range(4)):
            need("tensor", *w_ready["k"])
            need("tensor", s_d, padded)
            need("scalar", s_c, consts)
            for c in chunks:
                lo, w = CH[c]
                need("tensor", *ctx_ready[b][c])
                n, bank = job()
                mms = []
                for k in range(KT):
                    mms += three(bank[:, 0:w], wkh[:, k, :], wkl[:, k, :], ch[:, k, lo:lo + w], cl[:, k, lo:lo + w])
                matmuls(mms, s_w)
                need("scalar", s_w, filled(n))
                bias = bkv_sb[:, kv:kv + 1]
                hi, src = kh[:, lo:lo + w], bank[:, 0:w]
                need("vector", s_h, do("scalar", lambda e, hi=hi, src=src, bias=bias: e.activation(
                    hi, src, ACT.Identity, bias=bias), s_h))
                do("vector", lambda e, hi=hi, lo_=kl[:, lo:lo + w], src=src, bias=bias: e.scalar_tensor_tensor(
                    lo_, src, bias, f32(hi), ALU.add, ALU.subtract), s_f)
                emptied(n)
                k_ready[c] = s_f.n
            last_use["k"] = s_w.n
            last_use["ctx"] = s_w.n

        def proj_v(b, p, groups):
            need("tensor", *ctx_ready[b][3])
            need("tensor", *w_ready["v"])
            for g in groups:
                ts = range(2 * g, min(2 * g + 2, NT))
                n, bank = job()
                for t in ts:
                    rows = min(128, LK - 128 * t)
                    mms = []
                    for k in range(KT):
                        ps = slice(128 * t, 128 * t + rows)
                        mms += three(bank[0:rows, (t - 2 * g) * 256:(t - 2 * g + 1) * 256], ch[:, k, ps], cl[:, k, ps],
                                     wvh[:, k, :], wvl[:, k, :])
                    matmuls(mms, s_w if t == ts[-1] else None)
                m = len(ts)
                src = bank[0:rows, 0:256 * m].rearrange("p (t c) -> p t c", t=m)
                hi, lo = (a[0:rows, 2 * g:2 * g + m, :] for a in (vh, vl))
                need("scalar", s_w, filled(n))
                need("vector", s_h, do("scalar", lambda e, hi=hi, src=src: e.activation(hi, src, ACT.Copy), s_h))
                do("vector", lambda e, hi=hi, lo=lo, src=src: e.tensor_tensor(lo, src, f32(hi), ALU.subtract), s_f)
                emptied(n)
            v_ready["f"] = s_f.n
            last_use["v"] = s_w.n
            last_use["ctx"] = s_w.n

        def proj_q(b, u, h):
            need("tensor", *w_ready["q"])
            need("tensor", s_f, xt_ready[b])
            n, bank = job()
            mms = []
            for k in range(KT):
                ws = slice(h * 128, (h + 1) * 128)
                mms += three(bank[:, 0:256], wqh[:, k, ws], wql[:, k, ws], xth[:, k, :], xtl[:, k, :])
            matmuls(mms, s_w)
            need("scalar", s_w, filled(n))
            need("scalar", s_d, scaled_bq)
            bias = bq_sb[:, 2 * u + h:2 * u + h + 1]
            hi, lo = (a[:, h * 256:(h + 1) * 256] for a in (qh, ql))
            src = bank[:, 0:256]
            need("vector", s_h, do("scalar", lambda e: e.activation(hi, src, ACT.Identity, bias=bias), s_h))
            do("vector", lambda e: e.scalar_tensor_tensor(lo, src, bias, f32(hi), ALU.add, ALU.subtract), s_f)
            emptied(n)
            q_ready[b * NU + u, h] = s_f.n
            last_use["q"] = s_w.n

        e_done = {}
        t_done = {}

        m_parts = {}
        m_done = {}

        def scores(i, parts=3):
            j, par = i % 4, i % 2
            need("tensor", s_f, q_ready[i // 4, j // 2])
            qs = slice(j * 128, (j + 1) * 128)
            need("tensor", s_f, max(k_ready.values()))
            for c, (lo, hi) in enumerate(SC):
                if i:
                    need("tensor", s_e, e_done[i - 1][c // 2])
                sv = matmuls(three(psS[:, OFF + lo:OFF + hi], qh[:, qs], ql[:, qs], kh[:, lo:hi], kl[:, lo:hi]), s_s)
                if c and parts == 3:
                    need("vector", s_s, sv)
                    lo, hi = 0 if c == 1 else lo, min(hi, LK)
                    m_parts[i] = do("vector", lambda e, c=c, lo=lo, hi=hi: e.tensor_reduce(
                        mx[:, par, c - 1:c], psS[:, OFF + lo:OFF + hi], X, ALU.max), s_d)
            if parts == 1:
                need("vector", s_s, sv)
                m_done[i] = do("vector", lambda e: e.tensor_reduce(
                    nm[:, par:par + 1], psS[:, OFF:OFF + LK], X, ALU.max, negate=True), s_nb)

        def greatest(i):
            par = i % 2
            need("vector", s_d, m_parts[i])
            m_done[i] = do("vector", lambda e: e.tensor_reduce(nm[:, par:par + 1], mx[:, par, :], X, ALU.max, negate=True),
                           s_nb)

        def exps(i, halves=(0, 1)):
            j, par, up = i % 4, i % 2, (i // 4) % 2
            need("scalar", s_nb, m_done[i])
            need("scalar", s_w, t_done.get(i - 2))
            if i >= 8:
                need("scalar", s_r, i // 4 - 1)
            e_done.setdefault(i, [])
            for c in halves:
                lo, hi = ((0, HALF), (HALF, LK))[c]
                e_done[i].append(do("scalar", lambda e, c=c, lo=lo, hi=hi: e.activation(
                    p_sb[:, par, lo:hi], psS[:, OFF + lo:OFF + hi], ACT.Exp, bias=nm[:, par:par + 1],
                    accum_out=sums[:, up, j, c:c + 1]), s_e))

        GROUPS = ((NT - 1, NT), (0, 4), (4, 8), (8, 12))
        split_at = {}

        def turn_p(i, groups=range(4), hooks={}):
            j, par = i % 4, i % 2
            cs = slice(j * 128, (j + 1) * 128)
            need("tensor", s_e, e_done[i][1])
            for q in groups:
                g, z = GROUPS[q]
                n, bank = job()
                rows = 128
                for t in range(g, z):
                    rows = min(128, LK - 128 * t)
                    do("tensor", lambda e, t=t, g=g, rows=rows, bank=bank: e.transpose(
                        bank[0:rows, (t - g) * 128:(t - g + 1) * 128], p_sb[:, par, 128 * t:128 * t + rows], ident[:, :]),
                       s_w if t == z - 1 else None)
                v = t_done[i] = filled(n)
                src = bank[0:rows, 0:128 * (z - g)].rearrange("p (t c) -> p t c", t=z - g)
                hi, lo = (a[0:rows, g:z, cs] for a in (pth, ptl))
                if ("before", q) in hooks:
                    hooks["before", q]()
                need("scalar", s_w, v)
                need("vector", s_h, do("scalar", lambda e, hi=hi, src=src: e.activation(hi, src, ACT.Copy), s_h))
                do("vector", lambda e, hi=hi, lo=lo, src=src: e.tensor_tensor(lo, src, f32(hi), ALU.subtract), s_f)
                emptied(n)
                split_at[i // 4, q] = s_f.n
                if ("after", q) in hooks:
                    hooks["after", q]()

        def inverse_sums(U):
            up = U % 2
            need("vector", s_e, e_done[4 * U + 3][1])
            if U >= 2:
                need("vector", s_rw, 16 * (U - 1))
            dve(lambda e: e.tensor_tensor(ssum[:, up, :], sums[:, up, :, 0], sums[:, up, :, 1], ALU.add))
            v = do("vector", lambda e: e.reciprocal(rinv[:, up, :], ssum[:, up, :]), s_r)
            need("sync", s_r, v)
            if U >= 2:
                need("sync", s_rr, 16 * (U - 1))
            v = do("sync", lambda e: e.dma_start(scr_r[up].rearrange("(t p) -> p t", p=128), rinv[:, up, :],
                                                 allow_slow_non_contiguous=True), s_rw, 16)
            need("sync", s_rw, v)
            if U:
                need("sync", s_f, normed[U - 1])
            do("sync", lambda e: e.dma_start(rbc[:, :], scr_r[up].partition_broadcast(128)), s_rr, 16)

        pv_job = {}
        normed = {}

        def values(U, between):
            need("tensor", s_f, v_ready["f"])
            hs = slice(128 * (U // 2 % 2), 128 * (U // 2 % 2) + 128)
            n, bank = job()
            k, total = 0, 3 * NT
            for q, (g, z) in enumerate(GROUPS):
                for t in range(g, z):
                    if t in between:
                        between[t]()
                    need("tensor", s_f, split_at[U, q])
                    rows = min(128, LK - 128 * t)
                    for a, p in ((vh, pth), (vh, ptl), (vl, pth)):
                        do("tensor", lambda e, a=a, p=p, t=t, rows=rows, k=k: e.matmul(
                            bank, a[0:rows, t, hs], p[0:rows, t, :], start=(k == 0), stop=(k == total - 1)),
                           s_w if k == total - 1 else None)
                        k += 1
            pv_job[U] = (filled(n), bank, n)

        def norm_o(U):
            v, bank, n = pv_job[U]
            need("vector", s_w, v)
            need("vector", s_rr, 16 * (U + 1))
            need("vector", s_oh, U)
            need("vector", s_ol, U)
            if U:
                need("vector", s_w, last_use["o"])
            v = do("vector", lambda e: e.tensor_tensor(on[:, :], bank, rbc[:, :], ALU.mult), s_f)
            normed[U] = v
            emptied(n)

        def upper_o(U):
            need("scalar", s_f, normed[U])
            if U:
                need("scalar", s_w, last_use["o"])
            bias = bkv_sb[:, 8 + U % NU // 2:9 + U % NU // 2]
            do("scalar", lambda e: e.activation(oh[:, :], on[:, :], ACT.Identity, bias=bias), s_oh)

        def rest_o(U):
            need("vector", s_oh, U + 1)
            bias = bkv_sb[:, 8 + U % NU // 2:9 + U % NU // 2]
            do("vector", lambda e: e.scalar_tensor_tensor(
                ol[:, :], on[:, :], bias, f32(oh[:, :]), ALU.add, ALU.subtract), s_ol)

        def proj_o(U, t):
            need("tensor", *w_ready["o"])
            need("tensor", s_ol, U + 1)
            n, bank = job()
            mms = []
            for h in range(2):
                cs = slice(h * 256 + t * 128, h * 256 + (t + 1) * 128)
                mms += three(bank, oh[:, cs], ol[:, cs], woh[:, h, :], wol[:, h, :])
            if U % NU == 0:
                need("tensor", s_d, bo_split)
                mms += [(bank, one_row, bo_lo), (bank, one_row, bo_hi)]
            matmuls(mms, s_w)
            last_use["o"] = s_w.n
            need("vector", s_w, filled(n))
            need("vector", s_acc, acc_ready[U // NU])
            need("vector", s_f, acc_at[t])
            acc_at[t] = do("vector", lambda e, t=t: e.scalar_tensor_tensor(
                acc[:, t, :], bank, tg[:, 0:1], acc[:, t, :], ALU.mult, ALU.add), s_f)
            emptied(n)

        acc_at = {0: 0, 1: 0}

        def store_acc(b):
            need("sync", s_f, max(acc_at.values()))
            do("sync", lambda e: e.dma_start(scr_x[:, 2 * b:2 * b + 2, :], acc[:, :, :]), s_st, 16)

        made = {}

        def ffn_load():
            need("sync", s_w, last_use["ctx"])
            need("sync", s_st, 16 * (B - 1))
            do("sync", lambda e: e.dma_start(x1[:, :, :], scr_x[:, 0:NQ - 2, :]), s_x1, 16)
            do("sync", lambda e: e.dma_start(la_sb[:, :, 0:128], la), s_fw, 16)
            do("sync", lambda e: e.dma_start(la_sb[:, :, 128:136], rw), s_fw, 16)
            do("sync", lambda e: e.dma_start(bw_sb[:, :, :], bw), s_fw, 16)
            do("sync", lambda e: e.dma_start(lb_sb[:, :], lb), s_fw, 16)
            need("gpsimd", s_w, last_use["ctx"])
            for e_ in range(E):
                made["rev"] = do("gpsimd", lambda e, e_=e_: e.memset(rev[:, e_:e_ + 1], float(E - e_)), s_id)

        def tile_of(i):
            return x1[:, i, :] if i < NQ - 2 else acc[:, i - (NQ - 2), :]

        def ffn_stats(ts):
            for t in ts:
                stats(t, tile_of(t), steps)

        turned_h = {}

        normed_h = {}

        def ffn_norm(i):
            need("vector", s_w, turned_h.get("w"))
            normed_h[i] = do("vector", lambda e: e.tensor_scalar(
                hn[:, :], tile_of(i), mv[:, i, 0:1], rstd[:, i:i + 1], ALU.subtract, ALU.mult), s_d)

        def ffn_turn(i):
            need("tensor", s_d, normed_h[i])
            n, bank = job()
            for k in range(KT):
                do("tensor", lambda e, k=k: e.transpose(bank[:, k * 128:(k + 1) * 128], hn[:, k * 128:(k + 1) * 128],
                                                        ident[:, :]), s_w if k == KT - 1 else None)
            turned_h["w"] = filled(n)
            need("vector", s_w, filled(n))
            turned_h[i] = do("vector", lambda e: e.tensor_copy(hT[:, i, :, :], bank.rearrange("p (k c) -> p k c", k=KT)),
                             s_f)
            emptied(n)

        mid_at = {}

        def ffn_mid(i):
            need("tensor", s_fw, 64)
            need("tensor", s_f, turned_h[i])
            n, bank = job()
            matmuls([(bank[:, 0:136], hT[:, i, k, :], la_sb[:, k, :]) for k in range(KT)], s_w)
            need("vector", s_w, filled(n))
            mid_at[i] = do("vector", lambda e: e.tensor_copy(mid[:, i, :], bank[:, 0:136]), s_f)
            emptied(n)

        def route(a, z):
            shape = [128, z - a, E]
            bc = lambda ap: ap.unsqueeze(2).to_broadcast(shape)
            rv = rev[:, :].unsqueeze(1).to_broadcast(shape)
            R = lambda k: rt[:, k - 1, a:z, :] if k else mid[:, a:z, 128:136]
            S_ = lambda k: rs[:, k, a:z]
            need("vector", s_f, mid_at[z - 1])
            need("vector", s_id, made["rev"])
            dve(lambda e: e.tensor_reduce(S_(0), R(0), X, ALU.max))
            dve(lambda e: e.tensor_tensor(R(1), R(0), bc(S_(0)), ALU.subtract))
            need("scalar", s_d, s_d.n)
            need("vector", s_ex, do("scalar", lambda e: e.activation(R(2), R(1), ACT.Exp), s_ex))
            dve(lambda e: e.tensor_reduce(S_(1), R(2), X, ALU.add))
            dve(lambda e: e.reciprocal(S_(2), S_(1)))
            dve(lambda e: e.tensor_tensor(R(3), R(2), bc(S_(2)), ALU.mult))
            dve(lambda e: e.tensor_reduce(S_(3), R(3), X, ALU.max))
            dve(lambda e: e.tensor_tensor(R(4), R(3), bc(S_(3)), ALU.is_equal))
            dve(lambda e: e.tensor_tensor(R(4), R(4), rv, ALU.mult))
            dve(lambda e: e.tensor_reduce(S_(4), R(4), X, ALU.max))
            dve(lambda e: e.tensor_tensor(R(5), rv, bc(S_(4)), ALU.is_equal))
            dve(lambda e: e.scalar_tensor_tensor(R(6), R(5), -2.0, R(3), ALU.mult, ALU.add))
            dve(lambda e: e.tensor_reduce(S_(5), R(6), X, ALU.max))
            dve(lambda e: e.tensor_tensor(R(7), R(6), bc(S_(5)), ALU.is_equal))
            dve(lambda e: e.tensor_tensor(R(7), R(7), rv, ALU.mult))
            dve(lambda e: e.tensor_reduce(S_(6), R(7), X, ALU.max))
            dve(lambda e: e.tensor_tensor(R(8), rv, bc(S_(6)), ALU.is_equal))
            dve(lambda e: e.tensor_tensor(S_(7), S_(3), S_(5), ALU.add))
            dve(lambda e: e.reciprocal(S_(7), S_(7)))
            dve(lambda e: e.tensor_tensor(R(5), R(5), bc(S_(3)), ALU.mult))
            dve(lambda e: e.tensor_tensor(R(8), R(8), bc(S_(5)), ALU.mult))
            dve(lambda e: e.tensor_tensor(R(5), R(5), R(8), ALU.add))
            dve(lambda e: e.tensor_scalar(S_(7), S_(7), 2.0, None, ALU.mult))
            dve(lambda e: e.tensor_tensor(R(9), R(5), bc(S_(7)), ALU.mult))
            for i in range(a, z):
                inner = mid[:, i, 0:128].rearrange("p (e r) -> p e r", e=E)
                weighted[i] = do("vector", lambda e, i=i, inner=inner: e.tensor_tensor(
                    inner, inner, rt[:, 8, i, :].unsqueeze(2).to_broadcast([128, E, 16]), ALU.mult), s_d)

        weighted = {}

        gated = {}
        y_at = {}

        def ffn_gate(i):
            need("tensor", s_d, weighted[i])
            n, bank = job()
            do("tensor", lambda e: e.transpose(bank[:, 0:128], mid[:, i, 0:128], ident[:, :]), s_w)
            need("vector", s_w, filled(n))
            need("vector", s_w, y_at.get(i - 2))
            gated[i] = do("vector", lambda e: e.tensor_copy(midT[:, i % 2, :], bank[:, 0:128]), s_f)
            emptied(n)

        def ffn_y(i):
            need("tensor", s_f, gated[i])
            n, bank = job()
            mms = [(bank, hT[:, i, k, :], bw_sb[:, k, :]) for k in range(KT)]
            y_at[i] = matmuls(mms + [(bank, midT[:, i % 2, :], lb_sb[:, :])], s_w)
            need("vector", s_w, filled(n))
            v = do("vector", lambda e: e.scalar_tensor_tensor(
                tile_of(i), bank, tg[:, 1:2], tile_of(i), ALU.mult, ALU.add), s_f)
            emptied(n)
            need("sync", s_f, v)
            do("sync", lambda e: e.dma_start(out[:, i, :], tile_of(i)), s_out, 16)

        def fetch(name, dst, src):
            do("sync", lambda e: e.dma_start(dst, src), s_in[name], 16)
            return dst

        wk_raw = fetch("wk", lraw[:, 1024:1536], wk[0])
        c_raw = {}

        def fetch_ctx(c):
            lo, w = CH[c]
            w = min(w, LK - lo)
            c_raw[c] = fetch("c%d" % c, praw[:, KT * lo:KT * (lo + w)].rearrange("p (k c) -> p k c", k=KT),
                             ctxT[0, :, :, lo:lo + w])

        def split_ctx(c):
            lo, w = CH[c]
            w = min(w, LK - lo)
            for k in range(0, KT, 2):
                v = split_early(c_raw[c][:, k:k + 2, :], ch[:, k:k + 2, lo:lo + w], cl[:, k:k + 2, lo:lo + w], "c%d" % c)
            ctx_ready.setdefault(0, []).append(v)

        fetch_ctx(0)
        x_raw = fetch("x", lraw[:, 0:1024].rearrange("p (t c) -> p t c", t=2), x[:, 0:2, :])
        for c in range(1, 4):
            fetch_ctx(c)
        xr_raw = fetch("xr", lraw[:, 2560:5632].rearrange("p (t c) -> p t c", t=6), x[:, 2:8, :])
        fetch("bo", rbc[BO:BO + 1, :], bo.unsqueeze(0))
        start_acc(0)

        load_wq(0)
        load_wv(0)
        w_ready["k"] = split_early(wk_raw, flat(wkh), flat(wkl), "wk")
        split_ctx(0)
        split_ctx(1)
        proj_k(0, 0, [0])
        need("vector", s_in["x"], 16)
        for t in range(2):
            stats(t, x_raw[:, t, :], on)
        split_ctx(2)
        inverse_dev(0, 2, on)
        scaled_dev(0, 2)
        proj_k(0, 0, [1])
        for t in range(2):
            x_norm(t, x_raw[:, t, :], s_in["x"], 16)
        split_ctx(3)
        proj_k(0, 0, [2])
        for t in range(2):
            x_hat(0, t, x_raw[:, t, :])
        proj_k(0, 0, [3])
        proj_q(0, 0, 0)
        proj_q(0, 0, 1)
        load_wk(1)
        load_wq(1)
        scores(0)
        greatest(0)
        exps(0)
        need("vector", s_in["xr"], 16)
        for i in range(2, NQ):
            stats(i, xr_raw[:, i - 2, :], on)
        inverse_dev(2, NQ, on)
        scaled_dev(2, NQ)
        bo_hi, bo_lo, one_row = pth[BO:BO + 1, NT - 1, :], ptl[BO:BO + 1, NT - 1, :], vh[BO:BO + 1, NT - 1, 0:128]
        split_early(rbc[BO:BO + 1, :], bo_hi, bo_lo, "bo")
        bo_split = do("vector", lambda e: e.tensor_scalar(one_row, rbc[BO:BO + 1, 0:128], 0.0, 1.0, ALU.mult, ALU.add), s_d)
        proj_v(0, 0, range(4))
        scores(1)
        greatest(1)
        exps(1)
        load_wo(0)
        UN = B * NU
        for U in range(UN):
            b, u = divmod(U, NU)
            nb_, nu_ = divmod(U + 1, NU)
            more = U + 1 < UN
            kind, pair = u % 4, u // 4
            turning = u == 14 and b + 1 < B
            i = 4 * U

            if U:
                scores(i + 2, 1)
            else:
                proj_v(b, pair, (4,))
                turn_p(i)
                turn_p(i + 1, (0, 1))
                scores(i + 2, 1)
            if kind == 0 and U:
                proj_v(b, pair, (0,))
            turn_p(i + 1, (2, 3))
            exps(i + 2)
            if U:
                proj_o(U - 1, 0)
            if kind == 0:
                proj_v(b, pair, (5,) if U == 0 else (1, 2))
            if not more:
                ffn_turn(0)
                ffn_norm(1)
            if more:
                proj_q(nb_, nu_, 0)
            scores(i + 3)
            turn_p(i + 2, hooks={("after", 0): lambda: greatest(i + 3), ("before", 3): lambda: exps(i + 3)})
            if more:
                proj_q(nb_, nu_, 1)
                if turning:
                    x_hat(b + 1, 0, xraw[:, 0, :])
                if U + 2 < UN:
                    load_wq((nu_ + 1) % NU)
            if kind == 0:
                proj_v(b, pair, (6,) if U == 0 else (3, 4, 5, 6))
            if U:
                proj_o(U - 1, 1)
                if u == 0:
                    store_acc(b - 1)
                    start_acc(b)
                load_wo(u)
            if not more:
                ffn_turn(1)
                ffn_norm(2)
                ffn_mid(0)
            with_k = kind % 2 and more
            if with_k:
                proj_k(nb_, nu_ // 2, (0, 1))
                turn_p(i + 3, (0, 1))
                proj_k(nb_, nu_ // 2, (2,))
                turn_p(i + 3, (2,))
                proj_k(nb_, nu_ // 2, (3,))
                turn_p(i + 3, (3,))
            else:
                turn_p(i + 3)
            inverse_sums(U)
            if kind == 0 and pair < 3:
                load_wv(pair + 1)
            if u == 12 and b + 1 < B:
                x_hat_load(b + 1)
            if with_k and (nu_ // 2, nb_) != (7, B - 1):
                load_wk((nu_ // 2 + 1) % 8)
            if u == 13 and b + 1 < B:
                load_ctx(b + 1, range(2))
            if turning:
                load_ctx(b + 1, range(2, KT))
            if u == 13 and b == B - 1:
                ffn_load()
            def ahead_0():
                scores(i + 4)
                greatest(i + 4)
                exps(i + 4)
                if u == 13 and b + 1 < B:
                    for t in range(2):
                        x_norm(2 * b + 2 + t, xraw[:, t, :], s_x, 16 * (b + 1))
                if U == UN - 2:
                    need("vector", s_x1, 16)
                    ffn_stats((0, 1, 2))

            def ahead_1():
                turn_p(i + 4, (0, 1))
                scores(i + 5)
                greatest(i + 5)
                exps(i + 5, (0,))
                if U == UN - 2:
                    ffn_stats((3, 4, 5))

            def ahead_2():
                turn_p(i + 4, (2,))
                exps(i + 5, (1,))
                if U == UN - 2:
                    inverse_dev(0, NQ - 2, steps)
                    ffn_norm(0)
                if turning:
                    x_hat(b + 1, 1, xraw[:, 1, :])

            def feed_forward(turned, inner):
                def f():
                    if turned is not None:
                        ffn_turn(turned)
                        if turned < 5:
                            ffn_norm(turned + 1)
                        else:
                            route(0, 4)
                    if inner is not None:
                        ffn_mid(inner)
                return f

            if more:
                values(U, {1: ahead_0, 6: ahead_1, 8: ahead_2})
            else:
                values(U, {0: feed_forward(2, None), 1: feed_forward(None, 1), 2: feed_forward(3, None),
                           3: feed_forward(None, 2), 4: feed_forward(4, None), 6: feed_forward(None, 3),
                           7: feed_forward(5, None), 9: feed_forward(None, 4), 10: feed_forward(None, 5)})
            if turning:
                load_wv(0)
            if more:
                norm_o(U)
                turn_p(i + 5, (0, 1))
                turn_p(i + 4, (3,))
                upper_o(U)
                rest_o(U)
        norm_o(UN - 1)
        upper_o(UN - 1)
        ffn_gate(0)
        rest_o(UN - 1)
        ffn_gate(1)
        ffn_y(0)
        for t in range(2):
            proj_o(UN - 1, t)
        need("vector", s_f, max(acc_at.values()))
        ffn_stats((6, 7))
        inverse_dev(6, 8, steps)
        ffn_norm(6)
        ffn_gate(2)
        ffn_y(1)
        ffn_turn(6)
        ffn_norm(7)
        ffn_gate(3)
        ffn_y(2)
        ffn_mid(6)
        ffn_turn(7)
        route(4, 6)
        ffn_y(3)
        ffn_mid(7)
        ffn_gate(4)
        ffn_gate(5)
        route(6, 8)
        ffn_y(4)
        ffn_y(5)
        ffn_gate(6)
        ffn_gate(7)
        ffn_y(6)
        ffn_y(7)
        need("sync", s_out, s_out.n)
        need("sync", s_st, s_st.n)
        need("sync", s_rw, s_rw.n)

        @block.sync
        def _(eng):
            for f in queues["sync"]:
                f(eng)

        @block.gpsimd
        def _(eng):
            for f in queues["gpsimd"]:
                f(eng)

        @block.scalar
        def _(eng):
            for f in queues["scalar"]:
                f(eng)

        @block.vector
        def _(eng):
            for f in queues["vector"]:
                f(eng)

        @block.tensor
        def _(eng):
            for f in queues["tensor"]:
                f(eng)


def kernel(**inputs):
    import numpy as np
    import concourse.bacc as bacc
    from concourse.bass_utils import run_bass_kernel_spmd

    a = {k: np.asarray(v) for k, v in inputs.items()}
    B, LQ, D = a["x"].shape
    kt = D // 128
    wkv = a["L0_xattn_Wkv"]

    def by_column(w, n):
        c = w.shape[1] // n
        return w.reshape(kt, 128, n, c).transpose(2, 1, 0, 3).reshape(n, 128, kt * c)

    def by_row(w):
        return w.reshape(kt, 128, -1).transpose(1, 0, 2)

    E, _, R = a["L0_ffn_lora_A"].shape
    laid = {
        "x": a["x"].reshape(B * LQ // 128, 128, D).transpose(1, 0, 2),
        "ctxT": a["ctx_4096"].transpose(0, 2, 1).reshape(B, kt, 128, -1).transpose(0, 2, 1, 3),
        "gx": a["g_xattn"], "gf": a["g_ffn"],
        "wq": by_column(a["L0_xattn_Wq"], 16), "bq": a["L0_xattn_bq"].reshape(32, 128).T,
        "wk": by_column(wkv[:, :1024], 8), "wv": by_column(wkv[:, 1024:], 4),
        "bkv": a["L0_xattn_bkv"].reshape(16, 128).T,
        "wo": a["L0_xattn_Wo"].reshape(16, 2, 128, D).transpose(0, 2, 1, 3).reshape(16, 128, 2 * D),
        "bo": a["L0_xattn_bo"],
        "bw": by_row(a["L0_ffn_base_W"].T), "rw": by_row(a["L0_ffn_router_W"].T),
        "la": by_row(a["L0_ffn_lora_A"].transpose(1, 0, 2).reshape(D, E * R)),
        "lb": a["L0_ffn_lora_B"].reshape(E * R, D),
    }
    nc = bacc.Bacc("TRN2", target_bir_lowering=False, num_devices=1)
    f32 = mybir.dt.float32
    arrays, args = {}, []
    for name, v in laid.items():
        v = np.ascontiguousarray(v)
        arrays["in_" + name] = v
        args.append(nc.dram_tensor("in_" + name, v.shape, mybir.dt.from_np(v.dtype), kind="ExternalInput").ap())
    args.append(nc.dram_tensor("scr_r", (2, 512), f32, kind="Internal").ap())
    args.append(nc.dram_tensor("scr_x", (128, B * LQ // 128, D), f32, kind="Internal").ap())
    args.append(nc.dram_tensor("out_0", (128, B * LQ // 128, D), f32, kind="ExternalOutput").ap())
    gated_block(nc, *args)
    r = run_bass_kernel_spmd(nc, [arrays], core_ids=[0])
    y = r.results[0]["out_0"]
    return np.ascontiguousarray(y.transpose(1, 0, 2)).reshape(B, LQ, D)
```
